# Optimizing a Trainium2 kernel written in Bass

```python
import numpy as np
import jax
import jax.numpy as jnp

def _softmax(x, axis=-1):
    return jax.nn.softmax(x, axis=axis)

def _gelu(x):
    return jax.nn.gelu(x, approximate=True)

def _silu(x):
    return jax.nn.silu(x)

def _sigmoid(x):
    return jax.nn.sigmoid(x)

def _layernorm(x, axis=-1, eps=1e-05):
    m = jnp.mean(x, axis=axis, keepdims=True)
    v = jnp.var(x, axis=axis, keepdims=True)
    return (x - m) / jnp.sqrt(v + eps)

def _scatter_add(tgt, idx, src, axis=0):
    return tgt.at[idx].add(src)

def _segment_sum(src, seg, n):
    return jax.ops.segment_sum(src, seg, n)
kernel_name = 'mk_cond_seq_d4_seqx_r4_44f69a'

def setup_inputs(seed: int=0):
    np.random.seed(seed)
    _w = jnp.asarray

    def _rec_inputs():
        import jax
        import jax.numpy as jnp
        _rk = jax.random.key(seed)
        x = 7.22e-05 + 1 * jax.random.normal(jax.random.fold_in(_rk, 1), (16, 256, 256), jnp.float32)
        _lenS = 256 - jax.random.randint(jax.random.fold_in(_rk, 7), (16,), 0, max(1, 256 // 4) + 1, jnp.int32)
        _lenS2 = 256 - jax.random.randint(jax.random.fold_in(_rk, 8), (16,), 0, max(1, 256 // 4) + 1, jnp.int32)
        cond_1024 = 0.0061147 + 1.02565 * jax.random.normal(jax.random.fold_in(_rk, 11), (16, 256), jnp.float32)
        return (x, cond_1024)
    x, cond_1024 = _rec_inputs()

    def _L0_cond_setup():
        import jax, jax.numpy as jnp
        import numpy as np
        D = 256
        H = 16
        HKV = 4
        HD = D // H
        REP = H // HKV
        DFF = 1024
        B, N = (4, 512)
        EPS = 1e-05
        WSCALE = 0.02

        def _ln(x):
            m = jnp.mean(x, axis=-1, keepdims=True)
            v = jnp.mean(jnp.square(x - m), axis=-1, keepdims=True)
            return (x - m) * jax.lax.rsqrt(v + EPS)

        def _gqa_attn(h, wq, wk, wv, wo):
            b, n, d = h.shape
            q = (h @ wq.T).reshape(b, n, HKV, REP, HD)
            k = (h @ wk.T).reshape(b, n, HKV, HD)
            v = (h @ wv.T).reshape(b, n, HKV, HD)
            scores = jnp.einsum('bqgrh,bkgh->bgrqk', q, k) * (1.0 / np.sqrt(HD))
            a = jax.nn.softmax(scores, axis=-1)
            out = jnp.einsum('bgrqk,bkgh->bqgrh', a, v).reshape(b, n, d)
            return out @ wo.T

        def _mlp(h, w1, b1, w2, b2):
            h = jax.nn.gelu(h @ w1.T + b1, approximate=False)
            return h @ w2.T + b2
        key = jax.random.key(seed)
        ks = jax.random.split(key, 10)
        return {'x': jax.random.normal(ks[0], (B, N, D), jnp.float32), 'c': jax.random.normal(ks[1], (B, D), jnp.float32), 'wq': jax.random.normal(ks[2], (D, D), jnp.float32) * WSCALE, 'wk': jax.random.normal(ks[3], (HKV * HD, D), jnp.float32) * WSCALE, 'wv': jax.random.normal(ks[4], (HKV * HD, D), jnp.float32) * WSCALE, 'wo': jax.random.normal(ks[5], (D, D), jnp.float32) * WSCALE, 'w1': jax.random.normal(ks[6], (DFF, D), jnp.float32) * WSCALE, 'b1': jnp.zeros((DFF,), jnp.float32), 'w2': jax.random.normal(ks[7], (D, DFF), jnp.float32) * WSCALE, 'b2': jnp.zeros((D,), jnp.float32), 'wc': jax.random.normal(ks[8], (6 * D, D), jnp.float32) * WSCALE, 'bc': jnp.zeros((6 * D,), jnp.float32)}
    _L0_cond_all = _L0_cond_setup()
    _L0_cond_in = {k: v for k, v in _L0_cond_all.items() if k in ('wq', 'wk', 'wv', 'wo', 'w1', 'b1', 'w2', 'b2', 'wc', 'bc')}
    del _L0_cond_all

    def _L1_cond_setup():
        import jax, jax.numpy as jnp
        import numpy as np
        D = 256
        H = 16
        HD = 4 * D
        B, T = (4, 256)
        EPS = 1e-05

        def _layernorm(x, g, b):
            mu = jnp.mean(x, axis=-1, keepdims=True)
            var = jnp.mean(jnp.square(x - mu), axis=-1, keepdims=True)
            return (x - mu) * jax.lax.rsqrt(var + EPS) * g + b

        def _attention(x, Wqkv, Wproj, bproj):
            b, t, c = x.shape
            hd = c // H
            qkv = (x @ Wqkv).reshape(b, t, 3, H, hd).transpose(2, 0, 3, 1, 4)
            q, k, v = (qkv[0], qkv[1], qkv[2])
            scale = hd ** (-0.5)
            scores = jnp.einsum('bhqd,bhkd->bhqk', q, k) * scale
            causal = jnp.tril(jnp.ones((t, t), bool))
            scores = jnp.where(causal, scores, -jnp.inf)
            attn = jax.nn.softmax(scores, axis=-1)
            out = jnp.einsum('bhqk,bhkd->bhqd', attn, v)
            out = out.transpose(0, 2, 1, 3).reshape(b, t, c)
            return out @ Wproj + bproj
        key = jax.random.key(seed)
        ks = jax.random.split(key, 12)
        s = 0.02
        return {'x': jax.random.normal(ks[0], (B, T, D), jnp.float32), 'condition': jax.random.normal(ks[1], (B, D), jnp.float32), 'Wqkv': jax.random.normal(ks[2], (D, 3 * D), jnp.float32) * s, 'Wproj': jax.random.normal(ks[3], (D, D), jnp.float32) * s, 'bproj': jnp.zeros((D,), jnp.float32), 'W1': jax.random.normal(ks[4], (D, HD), jnp.float32) * s, 'b1': jnp.zeros((HD,), jnp.float32), 'W2': jax.random.normal(ks[5], (HD, D), jnp.float32) * s, 'b2': jnp.zeros((D,), jnp.float32), 'g1': jnp.ones((D,), jnp.float32), 'be1': jnp.zeros((D,), jnp.float32), 'g2': jnp.ones((D,), jnp.float32), 'be2': jnp.zeros((D,), jnp.float32), 'Wada': jax.random.normal(ks[6], (D, 6 * D), jnp.float32) * s, 'bada': jax.random.normal(ks[7], (6 * D,), jnp.float32) * s}
    _L1_cond_all = _L1_cond_setup()
    _L1_cond_in = {k: v for k, v in _L1_cond_all.items() if k in ('Wqkv', 'Wproj', 'bproj', 'W1', 'b1', 'W2', 'b2', 'g1', 'be1', 'g2', 'be2', 'Wada', 'bada')}
    del _L1_cond_all

    def _L2_cond_setup():
        import jax, jax.numpy as jnp
        import numpy as np
        D = 256
        H = 16
        HD = D // H
        MLP = 4 * D

        def _lin(key, fin, fout):
            k1, k2 = jax.random.split(key)
            lim = 1.0 / np.sqrt(fin)
            W = jax.random.uniform(k1, (fin, fout), minval=-lim, maxval=lim, dtype=jnp.float32)
            b = jax.random.uniform(k2, (fout,), minval=-lim, maxval=lim, dtype=jnp.float32)
            return (W, b)

        def layernorm(x, g, b, eps=1e-05):
            mu = jnp.mean(x, axis=-1, keepdims=True)
            var = jnp.var(x, axis=-1, keepdims=True)
            return (x - mu) * jax.lax.rsqrt(var + eps) * g + b

        def attention(h, Wqkv, bqkv, Wproj, bproj):
            B, L, _ = h.shape
            qkv = (h @ Wqkv + bqkv).reshape(B, L, 3, H, HD)
            q, k, v = jnp.moveaxis(qkv, 2, 0)
            scale = HD ** (-0.5)
            attn = jnp.einsum('blhd,bmhd->bhlm', q, k) * scale
            attn = jax.nn.softmax(attn, axis=-1)
            out = jnp.einsum('bhlm,bmhd->blhd', attn, v).reshape(B, L, D)
            return out @ Wproj + bproj
        key = jax.random.key(seed)
        ks = jax.random.split(key, 10)
        x = jax.random.normal(ks[0], (4, 512, D), dtype=jnp.float32)
        time_emb = jax.random.normal(ks[1], (4, D), dtype=jnp.float32)
        Wqkv, bqkv = _lin(ks[2], D, 3 * D)
        Wproj, bproj = _lin(ks[3], D, D)
        W1, b1 = _lin(ks[4], D, MLP)
        W2, b2 = _lin(ks[5], MLP, D)
        Wt, bt = _lin(ks[6], D, 6 * D)
        g1 = jnp.ones((D,), jnp.float32)
        be1 = jnp.zeros((D,), jnp.float32)
        g2 = jnp.ones((D,), jnp.float32)
        be2 = jnp.zeros((D,), jnp.float32)
        return {'x': x, 'time_emb': time_emb, 'Wqkv': Wqkv, 'bqkv': bqkv, 'Wproj': Wproj, 'bproj': bproj, 'W1': W1, 'b1': b1, 'W2': W2, 'b2': b2, 'Wt': Wt, 'bt': bt, 'g1': g1, 'be1': be1, 'g2': g2, 'be2': be2}
    _L2_cond_all = _L2_cond_setup()
    _L2_cond_in = {k: v for k, v in _L2_cond_all.items() if k in ('Wqkv', 'bqkv', 'Wproj', 'bproj', 'W1', 'b1', 'W2', 'b2', 'Wt', 'bt', 'g1', 'be1', 'g2', 'be2')}
    del _L2_cond_all

    def _L3_cond_setup():
        import jax, jax.numpy as jnp
        import numpy as np
        EPS = float(np.finfo(np.float32).eps)

        def _rmsnorm(x, g):
            return x * jax.lax.rsqrt(jnp.mean(x * x, axis=-1, keepdims=True) + EPS) * g

        def _silu(x):
            return x * jax.nn.sigmoid(x)

        def _swiglu(x):
            a, gate = jnp.split(x, 2, axis=-1)
            return a * _silu(gate)

        def _rope(x):
            T, hd = (x.shape[1], x.shape[-1])
            inv_freq = 1.0 / 10000.0 ** (jnp.arange(0, hd, 2, dtype=jnp.float32) / hd)
            ang = jnp.arange(T, dtype=jnp.float32)[:, None] * inv_freq[None, :]
            cos = jnp.cos(ang)[None, :, None, :]
            sin = jnp.sin(ang)[None, :, None, :]
            x0, x1 = (x[..., 0::2], x[..., 1::2])
            o0 = x0 * cos - x1 * sin
            o1 = x1 * cos + x0 * sin
            return jnp.stack([o0, o1], axis=-1).reshape(x.shape)

        def _mha(x, w_qkv, b_qkv, w_ao, b_ao, n_head):
            B, T, C = x.shape
            hd = C // n_head
            qkv = x @ w_qkv + b_qkv
            q, k, v = jnp.split(qkv, 3, axis=-1)
            q = _rope(q.reshape(B, T, n_head, hd)).transpose(0, 2, 1, 3)
            k = _rope(k.reshape(B, T, n_head, hd)).transpose(0, 2, 1, 3)
            v = v.reshape(B, T, n_head, hd).transpose(0, 2, 1, 3)
            attn = jnp.einsum('bhqd,bhkd->bhqk', q, k) * (1.0 / np.sqrt(hd))
            attn = jax.nn.softmax(attn, axis=-1)
            out = jnp.einsum('bhqk,bhkd->bhqd', attn, v)
            out = out.transpose(0, 2, 1, 3).reshape(B, T, C)
            return out @ w_ao + b_ao

        def _ffn(x, w_fc, b_fc, w_fo, b_fo):
            return _swiglu(x @ w_fc + b_fc) @ w_fo + b_fo
        key = jax.random.key(seed)
        ks = jax.random.split(key, 10)
        B, T, D, H = (2, 512, 256, 16)
        s = 0.02
        return {'x': jax.random.normal(ks[0], (B, T, D), jnp.float32), 'time_emb': jax.random.normal(ks[1], (B, D), jnp.float32), 'g1': jnp.ones((D,), jnp.float32), 'g2': jnp.ones((D,), jnp.float32), 'w_qkv': jax.random.normal(ks[2], (D, 3 * D), jnp.float32) * s, 'b_qkv': jnp.zeros((3 * D,), jnp.float32), 'w_ao': jax.random.normal(ks[3], (D, D), jnp.float32) * s, 'b_ao': jnp.zeros((D,), jnp.float32), 'w_fc': jax.random.normal(ks[4], (D, 8 * D), jnp.float32) * s, 'b_fc': jnp.zeros((8 * D,), jnp.float32), 'w_fo': jax.random.normal(ks[5], (4 * D, D), jnp.float32) * s, 'b_fo': jnp.zeros((D,), jnp.float32), 'w_t1': jax.random.normal(ks[6], (D, 2 * D), jnp.float32) * s, 'b_t1': jnp.zeros((2 * D,), jnp.float32), 'w_t2': jax.random.normal(ks[7], (D, 4 * D), jnp.float32) * s, 'b_t2': jnp.zeros((4 * D,), jnp.float32)}
    _L3_cond_all = _L3_cond_setup()
    _L3_cond_in = {k: v for k, v in _L3_cond_all.items() if k in ('g1', 'g2', 'w_qkv', 'b_qkv', 'w_ao', 'b_ao', 'w_fc', 'b_fc', 'w_fo', 'b_fo', 'w_t1', 'b_t1', 'w_t2', 'b_t2')}
    del _L3_cond_all
    return {'x': x, 'cond_1024': cond_1024, 'L0_cond_wq': _L0_cond_in['wq'], 'L0_cond_wk': _L0_cond_in['wk'], 'L0_cond_wv': _L0_cond_in['wv'], 'L0_cond_wo': _L0_cond_in['wo'], 'L0_cond_w1': _L0_cond_in['w1'], 'L0_cond_b1': _L0_cond_in['b1'], 'L0_cond_w2': _L0_cond_in['w2'], 'L0_cond_b2': _L0_cond_in['b2'], 'L0_cond_wc': _L0_cond_in['wc'], 'L0_cond_bc': _L0_cond_in['bc'], 'L1_cond_Wqkv': _L1_cond_in['Wqkv'], 'L1_cond_Wproj': _L1_cond_in['Wproj'], 'L1_cond_bproj': _L1_cond_in['bproj'], 'L1_cond_W1': _L1_cond_in['W1'], 'L1_cond_b1': _L1_cond_in['b1'], 'L1_cond_W2': _L1_cond_in['W2'], 'L1_cond_b2': _L1_cond_in['b2'], 'L1_cond_g1': _L1_cond_in['g1'], 'L1_cond_be1': _L1_cond_in['be1'], 'L1_cond_g2': _L1_cond_in['g2'], 'L1_cond_be2': _L1_cond_in['be2'], 'L1_cond_Wada': _L1_cond_in['Wada'], 'L1_cond_bada': _L1_cond_in['bada'], 'L2_cond_Wqkv': _L2_cond_in['Wqkv'], 'L2_cond_bqkv': _L2_cond_in['bqkv'], 'L2_cond_Wproj': _L2_cond_in['Wproj'], 'L2_cond_bproj': _L2_cond_in['bproj'], 'L2_cond_W1': _L2_cond_in['W1'], 'L2_cond_b1': _L2_cond_in['b1'], 'L2_cond_W2': _L2_cond_in['W2'], 'L2_cond_b2': _L2_cond_in['b2'], 'L2_cond_Wt': _L2_cond_in['Wt'], 'L2_cond_bt': _L2_cond_in['bt'], 'L2_cond_g1': _L2_cond_in['g1'], 'L2_cond_be1': _L2_cond_in['be1'], 'L2_cond_g2': _L2_cond_in['g2'], 'L2_cond_be2': _L2_cond_in['be2'], 'L3_cond_g1': _L3_cond_in['g1'], 'L3_cond_g2': _L3_cond_in['g2'], 'L3_cond_w_qkv': _L3_cond_in['w_qkv'], 'L3_cond_b_qkv': _L3_cond_in['b_qkv'], 'L3_cond_w_ao': _L3_cond_in['w_ao'], 'L3_cond_b_ao': _L3_cond_in['b_ao'], 'L3_cond_w_fc': _L3_cond_in['w_fc'], 'L3_cond_b_fc': _L3_cond_in['b_fc'], 'L3_cond_w_fo': _L3_cond_in['w_fo'], 'L3_cond_b_fo': _L3_cond_in['b_fo'], 'L3_cond_w_t1': _L3_cond_in['w_t1'], 'L3_cond_b_t1': _L3_cond_in['b_t1'], 'L3_cond_w_t2': _L3_cond_in['w_t2'], 'L3_cond_b_t2': _L3_cond_in['b_t2']}

def reference(x, cond_1024, L0_cond_wq, L0_cond_wk, L0_cond_wv, L0_cond_wo, L0_cond_w1, L0_cond_b1, L0_cond_w2, L0_cond_b2, L0_cond_wc, L0_cond_bc, L1_cond_Wqkv, L1_cond_Wproj, L1_cond_bproj, L1_cond_W1, L1_cond_b1, L1_cond_W2, L1_cond_b2, L1_cond_g1, L1_cond_be1, L1_cond_g2, L1_cond_be2, L1_cond_Wada, L1_cond_bada, L2_cond_Wqkv, L2_cond_bqkv, L2_cond_Wproj, L2_cond_bproj, L2_cond_W1, L2_cond_b1, L2_cond_W2, L2_cond_b2, L2_cond_Wt, L2_cond_bt, L2_cond_g1, L2_cond_be1, L2_cond_g2, L2_cond_be2, L3_cond_g1, L3_cond_g2, L3_cond_w_qkv, L3_cond_b_qkv, L3_cond_w_ao, L3_cond_b_ao, L3_cond_w_fc, L3_cond_b_fc, L3_cond_w_fo, L3_cond_b_fo, L3_cond_w_t1, L3_cond_b_t1, L3_cond_w_t2, L3_cond_b_t2):
    import jax
    import jax.numpy as jnp

    def _L0_cond_ref(x, c, wq, wk, wv, wo, w1, b1, w2, b2, wc, bc):
        import jax, jax.numpy as jnp
        import numpy as np
        D = 256
        H = 16
        HKV = 4
        HD = D // H
        REP = H // HKV
        DFF = 1024
        B, N = (4, 512)
        EPS = 1e-05
        WSCALE = 0.02

        def _ln(x):
            m = jnp.mean(x, axis=-1, keepdims=True)
            v = jnp.mean(jnp.square(x - m), axis=-1, keepdims=True)
            return (x - m) * jax.lax.rsqrt(v + EPS)

        def _gqa_attn(h, wq, wk, wv, wo):
            b, n, d = h.shape
            q = (h @ wq.T).reshape(b, n, HKV, REP, HD)
            k = (h @ wk.T).reshape(b, n, HKV, HD)
            v = (h @ wv.T).reshape(b, n, HKV, HD)
            scores = jnp.einsum('bqgrh,bkgh->bgrqk', q, k) * (1.0 / np.sqrt(HD))
            a = jax.nn.softmax(scores, axis=-1)
            out = jnp.einsum('bgrqk,bkgh->bqgrh', a, v).reshape(b, n, d)
            return out @ wo.T

        def _mlp(h, w1, b1, w2, b2):
            h = jax.nn.gelu(h @ w1.T + b1, approximate=False)
            return h @ w2.T + b2
        cond = jax.nn.silu(c) @ wc.T + bc
        sh1, sc1, g1, sh2, sc2, g2 = jnp.split(cond, 6, axis=-1)
        sh1, sc1, g1 = (sh1[:, None], sc1[:, None], g1[:, None])
        sh2, sc2, g2 = (sh2[:, None], sc2[:, None], g2[:, None])
        h = _ln(x) * (1.0 + sc1) + sh1
        x = x + g1 * _gqa_attn(h, wq, wk, wv, wo)
        h = _ln(x) * (1.0 + sc2) + sh2
        x = x + g2 * _mlp(h, w1, b1, w2, b2)
        return x

    def _L1_cond_ref(x, condition, Wqkv, Wproj, bproj, W1, b1, W2, b2, g1, be1, g2, be2, Wada, bada):
        import jax, jax.numpy as jnp
        import numpy as np
        D = 256
        H = 16
        HD = 4 * D
        B, T = (4, 256)
        EPS = 1e-05

        def _layernorm(x, g, b):
            mu = jnp.mean(x, axis=-1, keepdims=True)
            var = jnp.mean(jnp.square(x - mu), axis=-1, keepdims=True)
            return (x - mu) * jax.lax.rsqrt(var + EPS) * g + b

        def _attention(x, Wqkv, Wproj, bproj):
            b, t, c = x.shape
            hd = c // H
            qkv = (x @ Wqkv).reshape(b, t, 3, H, hd).transpose(2, 0, 3, 1, 4)
            q, k, v = (qkv[0], qkv[1], qkv[2])
            scale = hd ** (-0.5)
            scores = jnp.einsum('bhqd,bhkd->bhqk', q, k) * scale
            causal = jnp.tril(jnp.ones((t, t), bool))
            scores = jnp.where(causal, scores, -jnp.inf)
            attn = jax.nn.softmax(scores, axis=-1)
            out = jnp.einsum('bhqk,bhkd->bhqd', attn, v)
            out = out.transpose(0, 2, 1, 3).reshape(b, t, c)
            return out @ Wproj + bproj
        mod = jax.nn.silu(condition) @ Wada + bada
        sh_a, sc_a, gt_a, sh_m, sc_m, gt_m = jnp.split(mod, 6, axis=1)
        xn = _layernorm(x, g1, be1)
        xm = xn * (1.0 + sc_a[:, None, :]) + sh_a[:, None, :]
        x = x + gt_a[:, None, :] * _attention(xm, Wqkv, Wproj, bproj)
        xn = _layernorm(x, g2, be2)
        xm = xn * (1.0 + sc_m[:, None, :]) + sh_m[:, None, :]
        h = jax.nn.gelu(xm @ W1 + b1, approximate=False)
        x = x + gt_m[:, None, :] * (h @ W2 + b2)
        return x

    def _L2_cond_ref(x, time_emb, Wqkv, bqkv, Wproj, bproj, W1, b1, W2, b2, Wt, bt, g1, be1, g2, be2):
        import jax, jax.numpy as jnp
        import numpy as np
        D = 256
        H = 16
        HD = D // H
        MLP = 4 * D

        def _lin(key, fin, fout):
            k1, k2 = jax.random.split(key)
            lim = 1.0 / np.sqrt(fin)
            W = jax.random.uniform(k1, (fin, fout), minval=-lim, maxval=lim, dtype=jnp.float32)
            b = jax.random.uniform(k2, (fout,), minval=-lim, maxval=lim, dtype=jnp.float32)
            return (W, b)

        def layernorm(x, g, b, eps=1e-05):
            mu = jnp.mean(x, axis=-1, keepdims=True)
            var = jnp.var(x, axis=-1, keepdims=True)
            return (x - mu) * jax.lax.rsqrt(var + eps) * g + b

        def attention(h, Wqkv, bqkv, Wproj, bproj):
            B, L, _ = h.shape
            qkv = (h @ Wqkv + bqkv).reshape(B, L, 3, H, HD)
            q, k, v = jnp.moveaxis(qkv, 2, 0)
            scale = HD ** (-0.5)
            attn = jnp.einsum('blhd,bmhd->bhlm', q, k) * scale
            attn = jax.nn.softmax(attn, axis=-1)
            out = jnp.einsum('bhlm,bmhd->blhd', attn, v).reshape(B, L, D)
            return out @ Wproj + bproj
        tp = (jax.nn.silu(time_emb) @ Wt + bt)[:, None, :]
        shift_msa, scale_msa, gate_msa, shift_mlp, scale_mlp, gate_mlp = jnp.split(tp, 6, axis=-1)
        h = layernorm(x, g1, be1)
        h = h * (1.0 + scale_msa) + shift_msa
        h = attention(h, Wqkv, bqkv, Wproj, bproj)
        x = x + gate_msa * h
        h = layernorm(x, g2, be2)
        h = h * (1.0 + scale_mlp) + shift_mlp
        h = jax.nn.gelu(h @ W1 + b1, approximate=False) @ W2 + b2
        x = x + gate_mlp * h
        return x

    def _L3_cond_ref(x, time_emb, g1, g2, w_qkv, b_qkv, w_ao, b_ao, w_fc, b_fc, w_fo, b_fo, w_t1, b_t1, w_t2, b_t2):
        import jax, jax.numpy as jnp
        import numpy as np
        EPS = float(np.finfo(np.float32).eps)

        def _rmsnorm(x, g):
            return x * jax.lax.rsqrt(jnp.mean(x * x, axis=-1, keepdims=True) + EPS) * g

        def _silu(x):
            return x * jax.nn.sigmoid(x)

        def _swiglu(x):
            a, gate = jnp.split(x, 2, axis=-1)
            return a * _silu(gate)

        def _rope(x):
            T, hd = (x.shape[1], x.shape[-1])
            inv_freq = 1.0 / 10000.0 ** (jnp.arange(0, hd, 2, dtype=jnp.float32) / hd)
            ang = jnp.arange(T, dtype=jnp.float32)[:, None] * inv_freq[None, :]
            cos = jnp.cos(ang)[None, :, None, :]
            sin = jnp.sin(ang)[None, :, None, :]
            x0, x1 = (x[..., 0::2], x[..., 1::2])
            o0 = x0 * cos - x1 * sin
            o1 = x1 * cos + x0 * sin
            return jnp.stack([o0, o1], axis=-1).reshape(x.shape)

        def _mha(x, w_qkv, b_qkv, w_ao, b_ao, n_head):
            B, T, C = x.shape
            hd = C // n_head
            qkv = x @ w_qkv + b_qkv
            q, k, v = jnp.split(qkv, 3, axis=-1)
            q = _rope(q.reshape(B, T, n_head, hd)).transpose(0, 2, 1, 3)
            k = _rope(k.reshape(B, T, n_head, hd)).transpose(0, 2, 1, 3)
            v = v.reshape(B, T, n_head, hd).transpose(0, 2, 1, 3)
            attn = jnp.einsum('bhqd,bhkd->bhqk', q, k) * (1.0 / np.sqrt(hd))
            attn = jax.nn.softmax(attn, axis=-1)
            out = jnp.einsum('bhqk,bhkd->bhqd', attn, v)
            out = out.transpose(0, 2, 1, 3).reshape(B, T, C)
            return out @ w_ao + b_ao

        def _ffn(x, w_fc, b_fc, w_fo, b_fo):
            return _swiglu(x @ w_fc + b_fc) @ w_fo + b_fo
        n_head = 16
        tp = _swiglu(time_emb @ w_t1 + b_t1) @ w_t2 + b_t2
        shift1, scale1, shift2, scale2 = jnp.split(tp, 4, axis=-1)
        h = _rmsnorm(x, g1) * (1.0 + scale1[:, None, :]) + shift1[:, None, :]
        x = x + _mha(h, w_qkv, b_qkv, w_ao, b_ao, n_head)
        h = _rmsnorm(x, g2) * (1.0 + scale2[:, None, :]) + shift2[:, None, :]
        x = x + _ffn(h, w_fc, b_fc, w_fo, b_fo)
        return x
    x = _L0_cond_ref(x, cond_1024, L0_cond_wq, L0_cond_wk, L0_cond_wv, L0_cond_wo, L0_cond_w1, L0_cond_b1, L0_cond_w2, L0_cond_b2, L0_cond_wc, L0_cond_bc)
    x = _L1_cond_ref(x, cond_1024, L1_cond_Wqkv, L1_cond_Wproj, L1_cond_bproj, L1_cond_W1, L1_cond_b1, L1_cond_W2, L1_cond_b2, L1_cond_g1, L1_cond_be1, L1_cond_g2, L1_cond_be2, L1_cond_Wada, L1_cond_bada)
    x = _L2_cond_ref(x, cond_1024, L2_cond_Wqkv, L2_cond_bqkv, L2_cond_Wproj, L2_cond_bproj, L2_cond_W1, L2_cond_b1, L2_cond_W2, L2_cond_b2, L2_cond_Wt, L2_cond_bt, L2_cond_g1, L2_cond_be1, L2_cond_g2, L2_cond_be2)
    x = _L3_cond_ref(x, cond_1024, L3_cond_g1, L3_cond_g2, L3_cond_w_qkv, L3_cond_b_qkv, L3_cond_w_ao, L3_cond_b_ao, L3_cond_w_fc, L3_cond_b_fc, L3_cond_w_fo, L3_cond_b_fo, L3_cond_w_t1, L3_cond_b_t1, L3_cond_w_t2, L3_cond_b_t2)
    return x

_drawn_inputs = setup_inputs


def setup_inputs(seed=0):
    import zlib

    import numpy as np

    out = dict(_drawn_inputs(seed))
    spreads = {'L0_cond_b1': (0.0, 0.8),
     'L0_cond_b2': (0.0, 0.393),
     'L0_cond_bc': (0.0, 0.512),
     'L1_cond_bproj': (0.0, 0.391),
     'L1_cond_b1': (0.0, 0.8),
     'L1_cond_b2': (0.0, 0.416),
     'L1_cond_g1': (1.0, 0.6),
     'L1_cond_be1': (0.0, 0.8),
     'L1_cond_g2': (1.0, 0.6),
     'L1_cond_be2': (0.0, 0.8),
     'L2_cond_g1': (1.0, 0.6),
     'L2_cond_be1': (0.0, 0.726),
     'L2_cond_g2': (1.0, 0.6),
     'L2_cond_be2': (0.0, 0.8),
     'L3_cond_g1': (1.0, 0.6),
     'L3_cond_g2': (1.0, 0.6),
     'L3_cond_b_qkv': (0.0, 0.1),
     'L3_cond_b_ao': (0.0, 0.79),
     'L3_cond_b_fc': (0.0, 0.499),
     'L3_cond_b_fo': (0.0, 2.0),
     'L3_cond_b_t1': (0.0, 0.8),
     'L3_cond_b_t2': (0.0, 0.65)}
    factors = {'L0_cond_wq': 8.0,
     'L0_cond_wk': 8.0,
     'L0_cond_wv': 8.0,
     'L0_cond_wo': 8.0,
     'L1_cond_Wqkv': 8.0,
     'L1_cond_Wproj': 8.0,
     'L1_cond_bada': 8.0,
     'L2_cond_bqkv': 7.524,
     'L2_cond_bproj': 4.402,
     'L2_cond_b1': 8.0,
     'L2_cond_b2': 8.0,
     'L2_cond_bt': 5.013,
     'L3_cond_w_qkv': 4.038,
     'L3_cond_w_t1': 8.0,
     'L3_cond_w_t2': 8.0}
    for name, (base, spread) in spreads.items():
        noise = np.random.default_rng([zlib.crc32(name.encode()), seed]).standard_normal(out[name].shape)
        drawn = base * np.exp(spread * noise) if base else spread * noise
        out[name] = jnp.asarray(drawn.astype(out[name].dtype))
    for name, factor in factors.items():
        out[name] = (out[name] * factor).astype(out[name].dtype)
    return out
```

```python
import numpy as np
import concourse.bass as bass
from concourse import mybir
from contextlib import ExitStack

F32 = mybir.dt.float32
F32R = mybir.dt.float32r
BF16 = mybir.dt.bfloat16
ALU = mybir.AluOpType
ACT = mybir.ActivationFunctionType
AX = mybir.AxisListType

P = 128
NL = 4
NSEQ = 16
T = 256
D = 256
H = 16
HD = D // H
DFF = 1024
NT = T // P
KD = D // P
NJ = DFF // P
HB = H // 2
STK = 48
ROWS = 64
RING = 4
STACKED = 16 * 12
PRING = 8
NTILE = NL * NSEQ
SCALE = HD ** -0.5
MASKED = -1.0e30
EPS = (1e-5, 1e-5, 1e-5, float(np.finfo(np.float32).eps))
CAUSAL, ROPE = 1, 3
QKV_BIAS = (False, False, True, True)
WQ_COLS = (3 * D, 3 * D, 3 * D, 5 * D)
W1_COLS = (DFF, DFF, DFF, 2 * DFF)
V_SC1, V_SH1, V_SC2, V_SH2, V_G1, V_BE1, V_G2, V_BE2, V_BQ, V_BK, V_BV, V_BQR, V_BKR = range(0, 26, 2)
V_B1 = 26
V_T1 = 42
NVEC = 46
C_S1, C_B1, C_S2, C_B2 = 0, 2, 4, 6
CHUNK = 1024


def build(nc, a, out):
    ctx = ExitStack()
    with ctx:
        def sb(name, shape, dt=F32):
            return ctx.enter_context(nc.sbuf_tensor(name, shape, dt))

        def sem(name):
            return ctx.enter_context(nc.semaphore(name))

        X = sb("X", [P, NSEQ, NT, D])
        IDENT = sb("IDENT", [P, P])
        IDENTB = sb("IDENTB", [P, P], BF16)
        MASK = sb("MASK", [P, 2, 2, T], BF16)
        ROT = sb("ROT", [P, 2, T])
        VEC = sb("VEC", [P, NL, NVEC])
        COND = sb("COND", [P, NL, 8, NSEQ])
        HALF = sb("HALF", [P, NT])
        WQ = [[sb(f"WQ{p}{x}", [P, KD, max(WQ_COLS[p::2])], F32R) for x in "hl"] for p in range(2)]
        WO = [sb(f"WO{x}", [P, KD, D], F32R) for x in "hl"]
        RAW = [sb(f"RAW{i}", [P, CHUNK // 2]) for i in range(2)]
        TOK = sb("TOK", [P, NT, D])
        ST1, ST2 = sb("ST1", [P, NT, 6]), sb("ST2", [P, NT, 6])
        MV1, MV2 = sb("MV1", [P, NT, 2]), sb("MV2", [P, NT, 2])
        RS1, RS2 = sb("RS1", [P, NT]), sb("RS2", [P, NT])
        TV = sb("TV", [P, NT])
        HF = sb("HF", [P, KD, T])
        H1 = [sb(f"H1{x}", [P, KD, T], F32R) for x in "hl"]
        H2 = [sb(f"H2{x}", [P, KD, T], F32R) for x in "hl"]
        QHL = sb("QHL", [P, 2, KD, T], F32R)
        KHL = sb("KHL", [P, 2, KD, T], F32R)
        QS = sb("QS", [P, HB, T], F32R)
        KS = sb("KS", [P, HB, T], F32R)
        V = sb("V", [P, NT, H, 32])
        NEGM = sb("NEGM", [P, NT, H])
        MT = sb("MT", [H, T], F32R)
        PR = sb("PR", [P, PRING, NT, T])
        OR = sb("OR", [P, 4, T])
        RZ = sb("RZ", [P, NT, H])
        G = sb("G", [P, RING, T])
        GH = [sb(f"GH{x}", [P, RING, T], F32R) for x in "hl"]
        GA = sb("GA", [P, 2, D])
        GM = sb("GM", [P, 2, D])
        B = ctx.enter_context(nc.psum_tensor("B", [P, 8, 512], F32))

        def bank(n, parts=2):
            return B[:, n, :].rearrange("p (a b) -> p a b", a=parts)

        sp_x, sp_const, sp_cw, sp_gs = sem("sp_x"), sem("sp_const"), sem("sp_cw"), sem("sp_gs")
        sp_raw = [sem("sp_raw0"), sem("sp_raw1")]
        sp_ga, sp_gm, sp_scr, sp_stk, sp_mt, sp_out = (sem("sp_" + x) for x in ("ga", "gm", "scr", "stk", "mt", "out"))
        pe_h1, pe_q, pe_k, pe_v, pe_s, pe_mt, pe_st, pe_pv, pe_ot1, pe_ot2, pe_wo, pe_h2, pe_up, pe_dn = (
            sem("pe_" + x) for x in ("h1", "q", "k", "v", "s", "mt", "st", "pv", "ot1", "ot2", "wo", "h2", "up", "dn"))
        ac_h1, ac_v, ac_mt, ac_exp, ac_o, ac_ot, ac_h2, ac_g, ac_w = (
            sem("ac_" + x) for x in ("h1", "v", "mt", "exp", "o", "ot", "h2", "g", "w"))
        dv_st1, dv_mv1, dv_xn1, dv_st2, dv_mv2, dv_xn2, dv_h1, dv_h2, dv_qh, dv_q, dv_kh, dv_k = (
            sem("dv_" + x) for x in ("st1", "mv1", "xn1", "st2", "mv2", "xn2", "h1", "h2", "qh", "q", "kh", "k"))
        dv_max, dv_rz, dv_on, dv_ot, dv_wo, dv_dn, dv_gh, dv_g, dv_rot, dv_rot2 = (
            sem("dv_" + x) for x in ("max", "rz", "on", "ot", "wo", "dn", "gh", "g", "rot", "rot2"))
        po_t1, po_rs1, po_t2, po_rs2, po_h1, po_h2, po_gl, po_xb1, po_x1, po_xb2, po_x2, po_w, po_init = (
            sem("po_" + x) for x in ("t1", "rs1", "t2", "rs2", "h1", "h2", "gl", "xb1", "x1", "xb2", "x2", "w", "init"))
        pc, cc, vc = sem("pe_cond"), sem("ac_cond"), sem("dv_cond")
        dv_init = sem("dv_init")

        q_scr = nc.dram_tensor("q_scratch", [2, P, KD, T], F32, kind="Internal").ap()
        k_scr = nc.dram_tensor("k_scratch", [2, P, KD, T], F32, kind="Internal").ap()
        g_scr = nc.dram_tensor("gate_scratch", [NL - 1, NSEQ, 4, D], F32, kind="Internal").ap()

        with ExitStack() as early:
            def esb(name, shape, dt=F32):
                return early.enter_context(nc.sbuf_tensor(name, shape, dt))

            CW = [esb(f"CW{l}", [P, KD, 6 * D]) for l in range(3)]
            CT1 = X[:, 8:10, :, :].rearrange("p s t d -> p s (t d)")
            CT2 = X[:, 10:14, :, :].rearrange("p (k s) t d -> p k (s t d)", k=KD)
            CT = esb("CT", [P, KD, NSEQ])
            SC = esb("SC", [P, KD, NSEQ])
            SLU = esb("SLU", [P, KD, NSEQ])
            Z3 = esb("Z3", [P, KD, NSEQ])
            U = esb("U", [P, 2, NSEQ])
            U2 = esb("U2", [P, 2, NSEQ])
            flat = PR[:].rearrange("p a b c -> p (a b c)")
            GR = flat[0:NSEQ, 0:12 * D].rearrange("p (l r d) -> p l r d", l=NL - 1, r=4)
            RB = [flat[0:NSEQ, 12 * D:16 * D].rearrange("p (r d) -> p r d", r=4), OR[0:NSEQ], G[0:NSEQ]]
            block = early.enter_context(nc.Block())
            ctile = bank(0, 32)
            t1tile = bank(1, 32)
            starts = [(D, 0, 4 * D, 3 * D)] * 3 + [(D, 0, 3 * D, 2 * D)]

            @block.sync
            def _(sp):
                sp.dma_start(CT[:], a["c_t"]).then_inc(sp_cw, 16)
                for l in range(3):
                    sp.dma_start(CW[l][:], a[f"cw{l}"].rearrange("(k p) n -> p k n", p=P)).then_inc(sp_cw, 16)
                sp.dma_start(CT1, a["cw_t1"].rearrange("(k p) n -> p k n", p=P)).then_inc(sp_cw, 16)
                sp.dma_start(CT2, a["cw_t2"].rearrange("(k p) n -> p k n", p=P)).then_inc(sp_cw, 16)
                sp.dma_start(VEC[:], a["vec"]).then_inc(sp_cw, 16)
                for l in range(3):
                    sp.dma_start(RB[l], a["rows"][l].partition_broadcast(NSEQ)).then_inc(sp_cw, 16)
                sp.dma_start(IDENT[:], a["ident"]).then_inc(sp_const, 16)
                sp.dma_start(ROT[:], a["rot"]).then_inc(sp_const, 16)
                sp.dma_start(MASK[:], a["mask"]).then_inc(sp_const, 16)
                sp.dma_start(IDENTB[:], a["ident_b"]).then_inc(sp_const, 16)
                x_in = a["x"].rearrange("s (t p) d -> p s t d", p=P)
                sp.dma_start(X[:, 0:8], x_in[:, 0:8]).then_inc(sp_x, 16)
                sp.wait_ge(vc, 10)
                sp.dma_start(g_scr.rearrange("l s r d -> s l r d"), GR).then_inc(sp_gs, 16)
                sp.wait_ge(pc, 5)
                sp.dma_start(X[:, 8:16], x_in[:, 8:16]).then_inc(sp_x, 16)
                sp.wait_ge(sp_gs, 16)
                sp.wait_ge(sp_x, 32)
                sp.wait_ge(sp_const, 64)

            @block.gpsimd
            def _(po):
                nc.gpsimd.memset(HALF[:], -0.5).then_inc(po_init, 1)
                nc.gpsimd.memset(QS[:].bitcast(F32), 0.0).then_inc(po_init, 1)
                nc.gpsimd.memset(KS[:].bitcast(F32), 1.0).then_inc(po_init, 1)
                nc.gpsimd.memset(V[:], 0.0).then_inc(po_init, 1)
                po.wait_ge(po_init, 4)
                nc.gpsimd.memset(V[:, :, :, HD:HD + 1], 1.0).then_inc(po_init, 1)
                po.wait_ge(po_init, 5)

            @block.scalar
            def _(ac):
                ac.wait_ge(sp_cw, 10 * 16)
                nc.scalar.activation(SC[:], CT[:], ACT.Silu).then_inc(cc, 1)
                ac.wait_ge(pc, 1)
                for k in range(KD):
                    nc.scalar.activation(SLU[:, k, :], t1tile[:, KD + k, :], ACT.Silu,
                                         bias=VEC[:, ROPE, V_T1 + KD + k:V_T1 + KD + k + 1]).then_inc(cc, 1)

            @block.tensor
            def _(pe):
                pe.wait_ge(sp_cw, 10 * 16)
                for f in range(2 * KD):
                    for k in range(KD):
                        last = nc.tensor.matmul(t1tile[:, f, :], CT1[:, k, f * P:(f + 1) * P], CT[:, k, :],
                                                start=(k == 0), stop=(k == KD - 1))
                last.then_inc(pc, 1)
                pe.wait_ge(cc, 1)
                for l in range(3):
                    for r, c0 in enumerate((2 * D, 5 * D)):
                        for k in range(KD):
                            last = nc.tensor.matmul(bank(2 + l)[0:NSEQ, r, :], SC[:, k, :], CW[l][:, k, c0:c0 + D],
                                                    start=(k == 0), stop=(k == KD - 1))
                    last.then_inc(pc, 1)
                for l in range(NL):
                    if l == ROPE:
                        pe.wait_ge(vc, 4)
                    w, m = (CT2, Z3) if l == ROPE else (CW[l], SC)
                    for c, c0 in enumerate(starts[l]):
                        for f in range(KD):
                            for k in range(KD):
                                last = nc.tensor.matmul(ctile[:, 8 * l + 2 * c + f, :],
                                                        w[:, k, c0 + f * P:c0 + (f + 1) * P], m[:, k, :],
                                                        start=(k == 0), stop=(k == KD - 1))
                last.then_inc(pc, 1)

            @block.vector
            def _(dv):
                n = [0]

                def chain(ins):
                    n[0] += 1
                    ins.then_inc(dv_init, 1)

                def settle():
                    dv.wait_ge(dv_init, n[0])

                dv.wait_ge(sp_cw, 10 * 16)
                dv.wait_ge(cc, 3)
                for k in range(KD):
                    nc.vector.scalar_tensor_tensor(Z3[:, k, :], t1tile[:, k, :], VEC[:, ROPE, V_T1 + k:V_T1 + k + 1],
                                                   SLU[:, k, :], ALU.add, ALU.mult).then_inc(vc, 2)
                for l in range(3):
                    dv.wait_ge(pc, 2 + l)
                    for r in range(2):
                        chain(nc.vector.tensor_tensor(GR[:, l, 2 * r, :], bank(2 + l)[0:NSEQ, r, :],
                                                      RB[l][:, 2 * r, :], ALU.add))
                settle()
                for l in range(3):
                    for r in range(2):
                        nc.vector.tensor_tensor(GR[:, l, 2 * r + 1, :], GR[:, l, 2 * r, :], RB[l][:, 2 * r + 1, :],
                                                ALU.mult).then_inc(vc, 1)
                dv.wait_ge(pc, 5)
                for l in range(NL):
                    for half, (sc, sh, g, be, cs, cb) in enumerate(((V_SC1, V_SH1, V_G1, V_BE1, C_S1, C_B1),
                                                                   (V_SC2, V_SH2, V_G2, V_BE2, C_S2, C_B2))):
                        for f in range(KD):
                            def vec(c):
                                return VEC[:, l, c + f:c + f + 1]
                            tile = 8 * l + 4 * half + f
                            chain(nc.vector.tensor_scalar(U[:, f, :], ctile[:, tile, :], vec(sc), 1.0, ALU.add, ALU.add))
                            chain(nc.vector.tensor_scalar(U2[:, f, :], ctile[:, tile + KD, :], vec(sh), None, ALU.add))
                            settle()
                            chain(nc.vector.tensor_scalar(COND[:, l, cs + f, :], U[:, f, :], vec(g), None, ALU.mult))
                            chain(nc.vector.scalar_tensor_tensor(COND[:, l, cb + f, :], U[:, f, :], vec(be), U2[:, f, :],
                                                                 ALU.mult, ALU.add))
                            settle()

        W1 = [sb(f"W1{x}", [P, KD, 2 * DFF], F32R) for x in "hl"]
        W2 = [sb(f"W2{x}", [P, NJ, D], F32R) for x in "hl"]

        HC = CHUNK // 2

        def chunks(l, what):
            if what == "q":
                v = a[f"wq{l}"].rearrange("(k p) n -> p k n", p=P)
                n = WQ_COLS[l]
                dst = WQ[l % 2]
            elif what == "o":
                v, n, dst = a[f"wo{l}"].rearrange("(k p) n -> p k n", p=P), D, WO
            elif what == "1":
                v, n, dst = a[f"w1{l}"].rearrange("(k p) n -> p k n", p=P), W1_COLS[l], W1
            else:
                v = a[f"w2{l}"].rearrange("(j p) n -> p j n", p=P)
                return [(v[:, j:j + 2, :], [w[:, j:j + 2, :] for w in W2], 2) for j in range(0, NJ, 2)]
            if what == "o":
                return [(v, [w[:] for w in dst], 2)]
            step = HC if n % HC == 0 else D
            return [(v[:, k, c:c + step], [w[:, k, c:c + step] for w in dst], 1)
                    for k in range(KD) for c in range(0, n, step)]

        order = []
        first = {}
        done = {}
        for l in range(NL):
            for what in "qo12":
                first[l, what] = len(order)
                order += chunks(l, what)
                done[l, what] = len(order)

        def raw_view(n):
            src, dst, parts = order[n]
            w = dst[0].free_size()
            v = RAW[n % 2][:, 0:w]
            return v.rearrange("p (a b) -> p a b", a=2) if parts == 2 else v

        class Step:

            def __init__(self, t, layer, last_q=False):
                fixed = isinstance(t, int)
                self.first = fixed and t == -1
                self.lq = (t + 1) // NSEQ if fixed else layer
                self.la = t // NSEQ if fixed else layer
                self.lm = (t - 1) // NSEQ if fixed else layer
                self.q = None if fixed and t + 1 >= NTILE else t + 1
                self.a = None if fixed and not 0 <= t < NTILE else t
                self.m = None if fixed and not 1 <= t <= NTILE else t - 1
                self.nq = min(t + 1, NTILE) if fixed else t + 1
                self.na = max(0, min(t, NTILE)) if fixed else t
                self.nm = max(0, t - 1) if fixed else t - 1
                self.q_done = self.nq + (self.q is not None)
                self.a_done = self.na + (self.a is not None)
                self.m_done = self.nm + (self.m is not None)
                self.sq = None if self.q is None else self.q - NSEQ * self.lq
                self.sa = None if self.a is None else self.a - NSEQ * self.la
                self.sm = None if self.m is None else self.m - NSEQ * self.lm
                self.conv_q = self.conv_o = self.conv_12 = None
                if fixed:
                    if t == -1:
                        self.conv_q = self.conv_o = self.conv_12 = 0
                    elif t >= 14 and (t + 2) % NSEQ == 0 and (t + 2) // NSEQ < NL:
                        self.conv_q = (t + 2) // NSEQ
                    elif t > 0 and t % NSEQ == 0 and t < NTILE:
                        self.conv_o = self.conv_12 = t // NSEQ

        def seq(s):
            return slice(s, s + 1) if isinstance(s, int) else bass.ds(s, 1)

        def at_least(eng, s, value):
            if not isinstance(value, int) or value > 0:
                eng.wait_ge(s, value)

        def apart(eng):
            eng.nop(nofuse=True)

        def steps(eng, body):
            for t in (-1, 0, 1):
                body(Step(t, 0))
            for l in range(NL):
                lo = NSEQ * l + 2
                with eng.Fori(lo, lo + 12) as t:
                    body(Step(t, l))
                for t in range(lo + 12, lo + 16 if l < NL - 1 else NTILE + 1):
                    body(Step(t, None))

        block = ctx.enter_context(nc.Block())

        @block.tensor
        def _(pe):
            def product(dst, w, x, first_k, last_k):
                for n, (i, j) in enumerate(((0, 0), (0, 1), (1, 0))):
                    last = nc.tensor.matmul(dst, w[i], x[j], start=(first_k and n == 0), stop=(last_k and n == 2))
                return last

            def project(dst, w, x):
                for k in range(KD):
                    last = product(dst, [v[:, k] for v in w], [v[:, k] for v in x], k == 0, k == KD - 1)
                return last

            def cols(w, c):
                return [v[:, :, c:c + P] for v in w]

            def weights(l, what):
                pe.wait_ge(ac_w, done[l, what])
                pe.wait_ge(po_w, done[l, what])

            def body(s):
                def scores(h):
                    a_, b = s.a, ROWS * (h // HB)
                    if h == 0:
                        pe.wait_ge(sp_stk, STACKED * (a_ + 1))
                        at_least(pe, dv_wo, s.na)
                    elif h == 1:
                        at_least(pe, dv_ot, s.na)
                        at_least(pe, ac_ot, s.na)
                    else:
                        pe.wait_ge(dv_max, H * a_ + h - 1)
                    for i in range(NT):
                        dst = bank(4 + h % 2)[:, i, :]
                        last = nc.tensor.matmul(dst, QS[b:b + STK, h % HB, i * P:(i + 1) * P], KS[b:b + STK, h % HB, :],
                                                start=True, stop=(s.la != CAUSAL))
                        if s.la == CAUSAL:
                            last = nc.tensor.matmul(dst, IDENTB[:], MASK[:, 0, i, :], start=False, stop=True)
                    last.then_inc(pe_s, 1)

                def up(j):
                    m = s.m
                    if j == 0:
                        weights(s.lm, "1")
                        pe.wait_ge(dv_h2, m + 1)
                        pe.wait_ge(po_h2, m + 1)
                        at_least(pe, ac_v, s.nq)
                    elif j == 1:
                        at_least(pe, dv_k, s.nq)
                    elif s.lm == ROPE:
                        pe.wait_ge(dv_g, NJ * (m - NSEQ * ROPE) + j - 1)
                    else:
                        pe.wait_ge(ac_g, NJ * m + j - 1)
                    if s.lm == ROPE:
                        project(bank(2 + j % 2)[:, 0, :], cols(W1, j * P), H2)
                        last = project(bank(2 + j % 2)[:, 1, :], cols(W1, DFF + j * P), H2)
                    else:
                        last = project(bank(2 + j % 2)[:, 0, :], cols(W1, j * P), H2)
                    last.then_inc(pe_up, 1)

                def down(j):
                    m = s.m
                    if j == 0:
                        weights(s.lm, "2")
                        at_least(pe, ac_o, 2 * s.na)
                    pe.wait_ge(dv_gh, NJ * m + j + 1)
                    pe.wait_ge(po_gl, NJ * m + j + 1)
                    for i in range(NT):
                        for n, (x, y) in enumerate(((0, 0), (0, 1), (1, 0))):
                            last = nc.tensor.matmul(bank(7)[:, i, :], GH[x][:, j % RING, i * P:(i + 1) * P],
                                                    W2[y][:, j, :], start=(j == 0 and n == 0 and i == 0),
                                                    stop=(j == NJ - 1 and n == 2), skip_group_check=True)
                    last.then_inc(pe_dn, 1)

                for h in range(H):
                    if s.a is not None:
                        scores(h)
                    if h == 4 and s.q is not None:
                        pe.wait_ge(dv_xn1, s.q + 1)
                        at_least(pe, ac_h2, s.na)
                        for f in range(KD):
                            for i in range(NT):
                                last = nc.tensor.transpose(bank(0)[:, f, i * P:(i + 1) * P],
                                                           TOK[:, i, f * P:(f + 1) * P], IDENT[:])
                        last.then_inc(pe_h1, 1)
                    if s.m is not None:
                        if 2 <= h < 2 + NJ:
                            up(h - 2)
                        if h >= H - NJ:
                            down(h - (H - NJ))
                if s.q is not None:
                    wq, rope = WQ[s.lq % 2], s.lq == ROPE
                    weights(s.lq, "q")
                    pe.wait_ge(dv_h1, s.q + 1)
                    pe.wait_ge(po_h1, s.q + 1)
                    at_least(pe, dv_on, 2 * s.na)
                    for f in range(KD):
                        last = project(bank(1)[:, f, :], cols(wq, f * P), H1)
                    if rope:
                        for f in range(KD):
                            last = project(bank(0)[:, f, :], cols(wq, 3 * D + f * P), H1)
                    last.then_inc(pe_q, 1)
                if s.a is not None:
                    pe.wait_ge(dv_max, H * s.a + H)
                    at_least(pe, ac_o, 2 * s.na)
                    for i in range(NT):
                        last = nc.tensor.transpose(B[0:H, 6, i * P:(i + 1) * P], NEGM[:, i, :], IDENT[:])
                    last.then_inc(pe_mt, 1)
                if s.q is not None:
                    if s.m is not None:
                        if s.lm == ROPE:
                            pe.wait_ge(dv_g, NJ * (s.m - NSEQ * ROPE) + NJ)
                        else:
                            pe.wait_ge(ac_g, NJ * s.m + NJ)
                    at_least(pe, ac_v, s.nq)
                    at_least(pe, dv_k, s.nq)
                    for f in range(KD):
                        last = project(bank(3)[:, f, :], cols(wq, D + f * P), H1)
                    if rope:
                        for f in range(KD):
                            last = project(bank(2)[:, f, :], cols(wq, 4 * D + f * P), H1)
                    last.then_inc(pe_k, 1)

                if s.a is not None:
                    a_ = s.a

                    def outputs(g):
                        pe.wait_ge(ac_exp, H * a_ + 4 * g + 4)
                        if g == 0:
                            pe.wait_ge(ac_v, a_ + 1)
                            pe.wait_ge(ac_mt, a_ + 1)
                        if g == 2:
                            at_least(pe, dv_dn, s.m_done)
                        for k in range(NT):
                            for j in range(4):
                                h = 4 * g + j
                                last = nc.tensor.matmul(bank(6 + g // 2)[32 * j:32 * j + 32, g % 2, :],
                                                        V[:, k, h, :], PR[:, h % PRING, k, :],
                                                        start=(k == 0), stop=(k == NT - 1))
                        last.then_inc(pe_pv, 1)

                    pe.wait_ge(sp_mt, 32 * (a_ + 1))
                    for h in range(H):
                        b = ROWS * (h // HB)
                        if h >= 2:
                            pe.wait_ge(ac_exp, H * a_ + h - 1)
                        for k in range(NT):
                            dst = bank(4 + h % 2)[:, k, :]
                            last = nc.tensor.matmul(dst, KS[b:b + ROWS, h % HB, k * P:(k + 1) * P],
                                                    QS[b:b + ROWS, h % HB, :], start=True, stop=(s.la != CAUSAL))
                            if s.la == CAUSAL:
                                last = nc.tensor.matmul(dst, IDENTB[:], MASK[:, 1, k, :], start=False, stop=True)
                        last.then_inc(pe_st, 1)
                        if h % 4 == 2 and h > 4:
                            outputs(h // 4 - 1)
                    outputs(3)
                if s.q is not None:
                    if rope:
                        pe.wait_ge(dv_k, s.q + 1)
                    for i in range(NT):
                        for k in range(KD):
                            last = product(bank(2)[:, i, :], [x[:, k, i * P:(i + 1) * P] for x in H1],
                                           [w[:, k, 2 * D:3 * D] for w in wq], k == 0, k == KD - 1)
                    last.then_inc(pe_v, 1)
                if s.a is not None:
                    a_ = s.a
                    pe.wait_ge(ac_o, 2 * a_ + 2)
                    if s.q is not None:
                        pe.wait_ge(dv_q, s.q + 1)
                    else:
                        pe.wait_ge(ac_h2, s.na)
                        pe.wait_ge(dv_on, 2 * s.na)
                    for i in range(NT):
                        for g in range(4):
                            last = nc.tensor.transpose(bank(i, 4)[:, g, :], OR[:, g, i * P:(i + 1) * P], IDENT[:])
                        last.then_inc(pe_ot1, 1)
                    pe.wait_ge(ac_exp, H * a_ + H)
                    pe.wait_ge(dv_on, 2 * a_ + 2)
                    for f in range(KD):
                        for i in range(NT):
                            last = nc.tensor.transpose(bank(5)[:, f, i * P:(i + 1) * P],
                                                       TOK[:, i, f * P:(f + 1) * P], IDENT[:])
                    last.then_inc(pe_ot2, 1)
                    weights(s.la, "o")
                    pe.wait_ge(ac_ot, a_ + 1)
                    pe.wait_ge(dv_ot, a_ + 1)
                    for i in range(NT):
                        for k in range(KD):
                            last = product(bank(4)[:, i, :], [x[:, k, i * P:(i + 1) * P] for x in H2],
                                           [w[:, k, :] for w in WO], k == 0, k == KD - 1)
                    last.then_inc(pe_wo, 1)
                    pe.wait_ge(dv_xn2, a_ + 1)
                    for f in range(KD):
                        for i in range(NT):
                            last = nc.tensor.transpose(bank(0)[:, f, i * P:(i + 1) * P],
                                                       TOK[:, i, f * P:(f + 1) * P], IDENT[:])
                    last.then_inc(pe_h2, 1)

            steps(pe, body)

        @block.scalar
        def _(ac):
            def split_hi(l, what):
                for n in range(first[l, what], done[l, what]):
                    ac.wait_ge(sp_raw[n % 2], 16 * (n // 2 + 1))
                    nc.scalar.activation(order[n][1][0], raw_view(n), ACT.Copy).then_inc(ac_w, 1)

            def cond(s, layer, sequence, c):
                return COND[:, layer, c, seq(sequence)]

            def body(s):
                if s.first:
                    split_hi(0, "q")
                if s.m is not None:
                    m = s.m
                    for j in range(NJ):
                        ac.wait_ge(pe_up, NJ * m + j + 1)
                        bias = VEC[:, s.lm, V_B1 + j:V_B1 + j + 1]
                        if j == 0:
                            at_least(ac, dv_k, s.nq)
                        at_least(ac, dv_gh, NJ * m + j + 1 - RING)
                        at_least(ac, po_gl, NJ * m + j + 1 - RING)
                        if s.lm == ROPE:
                            nc.scalar.activation(G[:, j % RING, :], bank(2 + j % 2)[:, 1, :], ACT.Silu,
                                                 bias=VEC[:, ROPE, V_B1 + NJ + j:V_B1 + NJ + j + 1]).then_inc(ac_g, 1)
                        else:
                            nc.scalar.activation(G[:, j % RING, :], bank(2 + j % 2)[:, 0, :], ACT.Gelu,
                                                 bias=bias).then_inc(ac_g, 1)
                        if j == 3:
                            modulate_1(s)
                if s.m is None:
                    modulate_1(s)
                if s.a is not None:
                    a_ = s.a
                    ac.wait_ge(pe_mt, a_ + 1)
                    at_least(ac, sp_mt, 32 * s.na)
                    nc.scalar.activation(MT[:], B[0:H, 6, 0:T], ACT.Copy).then_inc(ac_mt, 1)
                    for h in range(H):
                        ac.wait_ge(pe_st, H * a_ + h + 1)
                        at_least(ac, pe_pv, 4 * a_ + h // 4 - 1)
                        nc.scalar.activation(PR[:, h % PRING, :, :], bank(4 + h % 2), ACT.Exp, scale=SCALE).then_inc(ac_exp, 1)
                        if h == 12:
                            evacuate(s, 0)
                    evacuate(s, 1)
                if s.q is not None:
                    ac.wait_ge(pe_v, s.q + 1)
                    at_least(ac, pe_pv, 4 * s.a_done)
                    nc.scalar.activation(V[:, :, :, 0:HD], B[:, 2, :].rearrange("p (i h d) -> p i h d", i=NT, h=H),
                                         ACT.Copy).then_inc(ac_v, 1)
                if s.first:
                    split_hi(0, "o")
                if s.a is not None:
                    a_ = s.a
                    ac.wait_ge(pe_ot2, a_ + 1)
                    at_least(ac, pe_up, NJ * s.m_done)
                    for f in range(KD):
                        if QKV_BIAS[s.la]:
                            last = nc.scalar.activation(H2[0][:, f, :], bank(5)[:, f, :], ACT.Identity,
                                                        bias=VEC[:, s.la, V_BV + f:V_BV + f + 1])
                        else:
                            last = nc.scalar.activation(H2[0][:, f, :], bank(5)[:, f, :], ACT.Copy)
                    last.then_inc(ac_ot, 1)
                    if s.conv_o is not None:
                        split_hi(s.conv_o, "o")
                    ac.wait_ge(pe_h2, a_ + 1)
                    ac.wait_ge(dv_h1, s.q_done)
                    ac.wait_ge(po_h1, s.q_done)
                    for f in range(KD):
                        last = nc.scalar.activation(HF[:, f, :], bank(0)[:, f, :], ACT.Identity,
                                                    bias=cond(s, s.la, s.sa, C_B2 + f), scale=cond(s, s.la, s.sa, C_S2 + f))
                    last.then_inc(ac_h2, 1)
                if s.conv_q is not None and not s.first:
                    split_hi(s.conv_q, "q")
                if s.conv_12 is not None:
                    split_hi(s.conv_12, "1")
                    split_hi(s.conv_12, "2")

            def evacuate(s, half):
                ac.wait_ge(pe_pv, 4 * s.a + 2 * half + 2)
                at_least(ac, pe_ot1, 2 * s.na)
                nc.scalar.activation(OR[:, 2 * half:2 * half + 2, :], bank(6 + half), ACT.Copy).then_inc(ac_o, 1)

            def modulate_1(s):
                if s.q is None:
                    return
                ac.wait_ge(pe_h1, s.q + 1)
                at_least(ac, dv_h2, s.na)
                at_least(ac, po_h2, s.na)
                for f in range(KD):
                    last = nc.scalar.activation(HF[:, f, :], bank(0)[:, f, :], ACT.Identity,
                                                bias=cond(s, s.lq, s.sq, C_B1 + f), scale=cond(s, s.lq, s.sq, C_S1 + f))
                last.then_inc(ac_h1, 1)

            steps(ac, body)

        @block.vector
        def _(dv):
            def statistics(x, st, mv, s_st, s_mv, n):
                for i in range(NT):
                    last = nc.vector.bn_stats(st[:, i, :], x[i])
                last.then_inc(s_st, 1)
                dv.wait_ge(s_st, n + 1)
                apart(dv)
                for i in range(NT):
                    last = nc.vector.bn_aggr(mv[:, i, :], st[:, i, :])
                last.then_inc(s_mv, 1)

            def normalise(x, mv, rs, s_xn, rms):
                for i in range(NT):
                    if rms:
                        last = nc.vector.tensor_scalar(TOK[:, i, :], x[i], rs[:, i:i + 1], None, ALU.mult)
                    else:
                        last = nc.vector.tensor_scalar(TOK[:, i, :], x[i], mv[:, i, 0:1], rs[:, i:i + 1],
                                                       ALU.subtract, ALU.mult)
                last.then_inc(s_xn, 1)

            def tokens(sequence):
                return [X[:, seq(sequence), i, :] for i in range(NT)]

            def body(s):
                def maximum(h):
                    a_ = s.a
                    dv.wait_ge(pe_s, H * a_ + h + 1)
                    if h == 0:
                        at_least(dv, pe_mt, s.na)
                    nc.vector.tensor_reduce(NEGM[:, :, h], bank(4 + h % 2), op=ALU.max, axis=AX.X,
                                            negate=True).then_inc(dv_max, 1)

                def hidden(j):
                    m = s.m
                    dv.wait_ge(ac_g, NJ * m + j + 1)
                    if s.lm == ROPE:
                        nc.vector.scalar_tensor_tensor(G[:, j % RING, :], bank(2 + j % 2)[:, 0, :],
                                                       VEC[:, ROPE, V_B1 + j:V_B1 + j + 1], G[:, j % RING, :],
                                                       ALU.add, ALU.mult).then_inc(dv_g, 1)
                        dv.wait_ge(dv_g, NJ * (m - NSEQ * ROPE) + j + 1)
                    at_least(dv, pe_dn, NJ * m + j + 1 - RING)
                    nc.vector.tensor_copy(GH[0][:, j % RING, :], G[:, j % RING, :]).then_inc(dv_gh, 1)

                def split_1():
                    dv.wait_ge(ac_h1, s.q + 1)
                    at_least(dv, pe_v, s.nq)
                    nc.vector.tensor_copy(H1[0][:], HF[:]).then_inc(dv_h1, 1)

                for h in range(H):
                    if s.q is not None and h == 0:
                        if s.lq == 0:
                            if s.first:
                                dv.wait_ge(sp_x, 16)
                        else:
                            dv.wait_ge(po_x2, s.q - (NSEQ - 1))
                        statistics(tokens(s.sq), ST1, MV1, dv_st1, dv_mv1, s.q)
                    if s.a is not None:
                        maximum(h)
                    if s.q is not None and h == 2:
                        dv.wait_ge(po_rs1, s.q + 1)
                        at_least(dv, pe_h2, s.na)
                        normalise(tokens(s.sq), MV1, RS1, dv_xn1, s.lq == ROPE)
                    if s.m is not None:
                        if 4 <= h < 4 + NJ:
                            hidden(h - 4)
                        if h == 8 and s.q is not None:
                            split_1()
                if s.q is not None and s.m is None:
                    split_1()
                if s.m is not None:
                    dv.wait_ge(pe_dn, NJ * s.m + NJ)
                    dv.wait_ge(pe_h1, s.q_done)
                    multiply(s, bank(7), GM, sp_gm, s.m, s.lm).then_inc(dv_dn, 1)
                if s.q is not None:
                    split_qk(s, pe_q, sp_scr, QHL, 1, 0, V_BQ, V_BQR, dv_qh, dv_q, 0)
                    split_qk(s, pe_k, sp_scr, KHL, 3, 2, V_BK, V_BKR, dv_kh, dv_k, 1)
                if s.a is not None:
                    a_ = s.a
                    at_least(dv, po_x2, s.m_done)
                    dv.wait_ge(pe_h1, s.q_done)
                    for i in range(NT):
                        dv.wait_ge(pe_ot1, 2 * a_ + i + 1)
                        heads = B[:, i, :].rearrange("p (h c) -> p h c", h=H)
                        nc.vector.reciprocal(RZ[:, i, :], heads[:, :, HD]).then_inc(dv_rz, 1)
                        dv.wait_ge(dv_rz, 2 * a_ + i + 1)
                        nc.vector.tensor_tensor(TOK[:, i, :].rearrange("p (h d) -> p h d", h=H), heads[:, :, 0:HD],
                                                RZ[:, i, :].unsqueeze(2).to_broadcast([P, H, HD]),
                                                ALU.mult).then_inc(dv_on, 1)
                    dv.wait_ge(ac_ot, a_ + 1)
                    if QKV_BIAS[s.la]:
                        for f in range(KD):
                            last = nc.vector.scalar_tensor_tensor(H2[1][:, f, :], bank(5)[:, f, :],
                                                                  VEC[:, s.la, V_BV + f:V_BV + f + 1],
                                                                  H2[0][:, f, :].bitcast(F32), ALU.add, ALU.subtract)
                    else:
                        last = nc.vector.tensor_tensor(H2[1][:], bank(5), H2[0][:].bitcast(F32), ALU.subtract)
                    last.then_inc(dv_ot, 1)
                    dv.wait_ge(pe_wo, a_ + 1)
                    multiply(s, bank(4), GA, sp_ga, a_, s.la).then_inc(dv_wo, 1)
                    dv.wait_ge(po_x1, a_ + 1)
                    statistics(tokens(s.sa), ST2, MV2, dv_st2, dv_mv2, a_)
                    dv.wait_ge(po_rs2, a_ + 1)
                    normalise(tokens(s.sa), MV2, RS2, dv_xn2, s.la == ROPE)
                    dv.wait_ge(ac_h2, a_ + 1)
                    nc.vector.tensor_copy(H2[0][:], HF[:]).then_inc(dv_h2, 1)

            def multiply(s, src, rows, s_rows, n, layer):
                if layer == ROPE:
                    return nc.vector.tensor_copy(TOK[:], src)
                dv.wait_ge(s_rows, 16 * (n + 1))
                return nc.vector.tensor_tensor(TOK[:], src, rows[:, 0:1, :].to_broadcast([P, NT, D]), ALU.mult)

            def split_qk(s, s_pe, s_free, dst, nbank, nswap, vb, vbr, s_hi, s_lo, which):
                dv.wait_ge(s_pe, s.q + 1)
                at_least(dv, s_free, 64 * s.nq)
                if s.lq == ROPE:
                    if s.m is not None:
                        dv.wait_ge(po_gl, NJ * s.m_done)
                    if which == 1:
                        dv.wait_ge(dv_q, s.q + 1)
                    r = s.q - NSEQ * ROPE
                    for c, nb, b in ((0, nbank, vb), (1, nswap, vbr)):
                        for f in range(KD):
                            last = nc.vector.scalar_tensor_tensor(G[:, 2 * c + f, :], bank(nb)[:, f, :],
                                                                  VEC[:, ROPE, b + f:b + f + 1], ROT[:, c, :],
                                                                  ALU.add, ALU.mult)
                    last.then_inc(dv_rot, 1)
                    dv.wait_ge(dv_rot, 2 * r + which + 1)
                    nc.vector.tensor_tensor(G[:, 0:2, :], G[:, 0:2, :], G[:, 2:4, :], ALU.add).then_inc(dv_rot2, 1)
                    dv.wait_ge(dv_rot2, 2 * r + which + 1)
                    nc.vector.tensor_copy(dst[:, 0], G[:, 0:2, :]).then_inc(s_hi, 1)
                    dv.wait_ge(s_hi, s.q + 1)
                    nc.vector.tensor_tensor(dst[:, 1], G[:, 0:2, :], dst[:, 0].bitcast(F32), ALU.subtract).then_inc(s_lo, 1)
                elif QKV_BIAS[s.lq]:
                    for f in range(KD):
                        last = nc.vector.tensor_scalar(dst[:, 0, f, :], bank(nbank)[:, f, :],
                                                       VEC[:, s.lq, vb + f:vb + f + 1], None, ALU.add)
                    last.then_inc(s_hi, 1)
                    dv.wait_ge(s_hi, s.q + 1)
                    for f in range(KD):
                        last = nc.vector.scalar_tensor_tensor(dst[:, 1, f, :], bank(nbank)[:, f, :],
                                                              VEC[:, s.lq, vb + f:vb + f + 1],
                                                              dst[:, 0, f, :].bitcast(F32), ALU.add, ALU.subtract)
                    last.then_inc(s_lo, 1)
                else:
                    nc.vector.tensor_copy(dst[:, 0], bank(nbank)).then_inc(s_hi, 1)
                    dv.wait_ge(s_hi, s.q + 1)
                    nc.vector.tensor_tensor(dst[:, 1], bank(nbank), dst[:, 0].bitcast(F32), ALU.subtract).then_inc(s_lo, 1)

            steps(dv, body)

        @block.gpsimd
        def _(po):
            def split_lo(l, what):
                for n in range(first[l, what], done[l, what]):
                    po.wait_ge(ac_w, n + 1)
                    nc.gpsimd.tensor_tensor(order[n][1][1], raw_view(n), order[n][1][0].bitcast(F32),
                                            ALU.subtract).then_inc(po_w, 1)

            def rstd(mv, rs, s_mv, s_t, s_rs, n, layer):
                po.wait_ge(s_mv, n + 1)
                if layer == ROPE:
                    nc.gpsimd.tensor_tensor(TV[:], mv[:, :, 0], mv[:, :, 0], ALU.mult).then_inc(s_t, 1)
                    po.wait_ge(s_t, n + 2 * (n - NSEQ * ROPE) + 1)
                    nc.gpsimd.tensor_tensor(TV[:], TV[:], mv[:, :, 1], ALU.add).then_inc(s_t, 1)
                    po.wait_ge(s_t, n + 2 * (n - NSEQ * ROPE) + 2)
                    apart(po)
                    nc.gpsimd.tensor_scalar(TV[:], TV[:], EPS[layer], None, ALU.add).then_inc(s_t, 1)
                    po.wait_ge(s_t, n + 2 * (n - NSEQ * ROPE) + 3)
                else:
                    apart(po)
                    nc.gpsimd.tensor_scalar(TV[:], mv[:, :, 1], EPS[layer], None, ALU.add).then_inc(s_t, 1)
                    po.wait_ge(s_t, n + 1)
                nc.gpsimd.tensor_tensor(rs[:], TV[:], HALF[:], ALU.pow).then_inc(s_rs, 1)

            def bias_rows(layer, n):
                return not (layer == 0 and n == 0)

            def body(s):
                if s.first:
                    split_lo(0, "q")
                if s.q is not None:
                    rstd(MV1, RS1, dv_mv1, po_t1, po_rs1, s.q, s.lq)
                if s.a is not None:
                    po.wait_ge(dv_xn1, s.a + 1)
                    x = X[:, seq(s.sa), :, :].rearrange("p a t d -> p (a t) d")
                    po.wait_ge(sp_ga, 16 * (s.a + 1))
                    apart(po)
                    nc.gpsimd.tensor_tensor(x, x, GA[:, 1:2, :].to_broadcast([P, NT, D]), ALU.add).then_inc(po_xb1, 1)
                if s.m is not None:
                    m = s.m
                    for j in range(NJ):
                        po.wait_ge(dv_gh, NJ * m + j + 1)
                        nc.gpsimd.tensor_tensor(GH[1][:, j % RING, :], G[:, j % RING, :], GH[0][:, j % RING, :].bitcast(F32),
                                                ALU.subtract).then_inc(po_gl, 1)
                        if j == 3:
                            low_1(s)
                    po.wait_ge(dv_xn2, m + 1)
                    xm = X[:, seq(s.sm), :, :].rearrange("p a t d -> p (a t) d")
                    po.wait_ge(sp_gm, 16 * (m + 1))
                    apart(po)
                    nc.gpsimd.tensor_tensor(xm, xm, GM[:, 1:2, :].to_broadcast([P, NT, D]), ALU.add).then_inc(po_xb2, 1)
                    po.wait_ge(po_xb2, m + 1)
                    po.wait_ge(dv_dn, m + 1)
                    apart(po)
                    nc.gpsimd.tensor_tensor(xm, xm, TOK[:], ALU.add).then_inc(po_x2, 1)
                else:
                    low_1(s)
                if s.first:
                    split_lo(0, "o")
                if s.a is not None:
                    if s.conv_o is not None:
                        split_lo(s.conv_o, "o")
                    po.wait_ge(po_xb1, s.a + 1)
                    po.wait_ge(dv_wo, s.a + 1)
                    apart(po)
                    nc.gpsimd.tensor_tensor(x, x, TOK[:], ALU.add).then_inc(po_x1, 1)
                    rstd(MV2, RS2, dv_mv2, po_t2, po_rs2, s.a, s.la)
                    po.wait_ge(ac_h2, s.a + 1)
                    po.wait_ge(dv_h2, s.a + 1)
                    nc.gpsimd.tensor_tensor(H2[1][:], HF[:], H2[0][:].bitcast(F32), ALU.subtract).then_inc(po_h2, 1)
                if s.conv_q is not None and not s.first:
                    split_lo(s.conv_q, "q")
                if s.conv_12 is not None:
                    split_lo(s.conv_12, "1")
                    split_lo(s.conv_12, "2")

            def low_1(s):
                if s.q is None:
                    return
                po.wait_ge(dv_h1, s.q + 1)
                nc.gpsimd.tensor_tensor(H1[1][:], HF[:], H1[0][:].bitcast(F32), ALU.subtract).then_inc(po_h1, 1)

            steps(po, body)

        @block.sync
        def _(sp):
            def hold(s, value):
                at_least(sp, s, value)
                apart(sp)

            def load_raw(l, what):
                for n in range(first[l, what], done[l, what]):
                    if n >= 2:
                        hold(po_w, n - 1)
                    sp.dma_start(raw_view(n), order[n][0]).then_inc(sp_raw[n % 2], 16)

            def rows(dst, layer, sequence, half):
                if layer == ROPE:
                    return dst[:], a["rows_last"][half].partition_broadcast(P)
                src = g_scr[layer, seq(sequence), 2 * half:2 * half + 2, :].rearrange("a r d -> (a r) d")
                return dst[:], src.partition_broadcast(P)

            def store(s, tile, sequence):
                hold(po_x2, tile + 1)
                o = out[seq(sequence), :, :].rearrange("a (t p) d -> p (a t) d", p=P)
                sp.dma_start(o, X[:, seq(sequence), :, :].rearrange("p a t d -> p (a t) d")).then_inc(sp_out, 16)

            def body(s):
                if s.first:
                    load_raw(0, "q")
                    load_raw(0, "o")
                elif s.conv_o is not None:
                    load_raw(s.conv_o, "o")
                if s.a is not None:
                    hold(dv_wo, s.na)
                    hold(po_xb1, s.na)
                    sp.dma_start(*rows(GA, s.la, s.sa, 0)).then_inc(sp_ga, 16)
                if s.m is not None:
                    hold(dv_dn, s.nm)
                    hold(po_xb2, s.nm)
                    sp.dma_start(*rows(GM, s.lm, s.sm, 1)).then_inc(sp_gm, 16)
                    if s.lm == ROPE and not (isinstance(s.m, int) and s.m == NSEQ * ROPE):
                        store(s, s.m - 1, s.sm - 1)
                if s.a is not None:
                    hold(ac_mt, s.a + 1)
                    for half in range(2):
                        row = ROWS * half + STK
                        sp.dma_start(QS[row:row + 1, :, :].bitcast(F32),
                                     MT[HB * half:HB * half + HB, :].bitcast(F32)).then_inc(sp_mt, 16)
                if s.q is not None:
                    hold(sp_stk, STACKED * s.nq)
                    for w, (s_dv, src, scr) in enumerate(((dv_q, QHL, q_scr), (dv_k, KHL, k_scr))):
                        hold(s_dv, s.q + 1)
                        for x in range(2):
                            sp.dma_start(scr[x], src[:, x].bitcast(F32)).then_inc(sp_scr, 16)
                    hold(sp_scr, 64 * (s.q + 1))
                    hold(pe_st, H * s.a_done)
                    for scr, dst, ranks in ((q_scr, QS, (0, 1, 0)), (k_scr, KS, (0, 0, 1))):
                        for half in range(2):
                            v = scr[:, :, half, :].rearrange("x (h d) n -> x d h n", h=HB)
                            b = ROWS * half
                            for r, x in enumerate(ranks):
                                sp.dma_start(dst[b + HD * r:b + HD * r + HD, :, :].bitcast(F32), v[x]).then_inc(sp_stk, 16)
                if s.conv_q is not None and not s.first:
                    load_raw(s.conv_q, "q")
                if s.conv_12 is not None:
                    hold(pe_up, NJ * s.m_done)
                    hold(pe_dn, NJ * s.m_done)
                    load_raw(s.conv_12, "1")
                    load_raw(s.conv_12, "2")

            steps(sp, body)
            store(None, NTILE - 1, NSEQ - 1)
            sp.wait_ge(sp_out, 16 * NSEQ)


def lay_out(i):
    g = {k: np.asarray(v) for k, v in i.items()}
    d = {"x": g["x"]}

    def cols(v):
        return np.asarray(v).reshape(-1, P).T

    d["c_t"] = np.ascontiguousarray(g["cond_1024"].T.reshape(KD, P, NSEQ).transpose(1, 0, 2))
    d["cw0"], d["cw1"], d["cw2"] = g["L0_cond_wc"].T, g["L1_cond_Wada"], g["L2_cond_Wt"]
    d["cw_t1"], d["cw_t2"] = g["L3_cond_w_t1"], g["L3_cond_w_t2"]
    rep = H // 4

    def spread(w):
        return np.repeat(w.T.reshape(D, 4, 1, HD), rep, axis=2).reshape(D, D)

    swap = np.arange(D).reshape(-1, 2)[:, ::-1].reshape(-1)
    w3 = g["L3_cond_w_qkv"]
    d["wq0"] = np.concatenate([g["L0_cond_wq"].T, spread(g["L0_cond_wk"]), spread(g["L0_cond_wv"])], axis=1)
    d["wq1"], d["wq2"] = g["L1_cond_Wqkv"], g["L2_cond_Wqkv"]
    d["wq3"] = np.concatenate([w3, w3[:, 0:D][:, swap], w3[:, D:2 * D][:, swap]], axis=1)
    d["wo0"], d["wo1"], d["wo2"], d["wo3"] = g["L0_cond_wo"].T, g["L1_cond_Wproj"], g["L2_cond_Wproj"], g["L3_cond_w_ao"]
    d["w10"], d["w11"], d["w12"], d["w13"] = g["L0_cond_w1"].T, g["L1_cond_W1"], g["L2_cond_W1"], g["L3_cond_w_fc"]
    d["w20"], d["w21"], d["w22"], d["w23"] = g["L0_cond_w2"].T, g["L1_cond_W2"], g["L2_cond_W2"], g["L3_cond_w_fo"]

    one, none = np.ones(D, np.float32), np.zeros(D, np.float32)
    vec = np.zeros((P, NL, NVEC), np.float32)

    def put(l, c, v):
        v = cols(v)
        vec[:, l, c:c + v.shape[1]] = v

    mod = [g["L0_cond_bc"], g["L1_cond_bada"], g["L2_cond_bt"]]
    for l in range(3):
        b = mod[l].reshape(6, D)
        for c, v in ((V_SH1, b[0]), (V_SC1, b[1]), (V_SH2, b[3]), (V_SC2, b[4])):
            put(l, c, v)
    b = g["L3_cond_b_t2"].reshape(4, D)
    for c, v in ((V_SH1, b[0]), (V_SC1, b[1]), (V_SH2, b[2]), (V_SC2, b[3])):
        put(3, c, v)
    norms = [(one, none, one, none)] + [tuple(g[f"L{l}_cond_{n}"] for n in ("g1", "be1", "g2", "be2")) for l in (1, 2)] + [
        (g["L3_cond_g1"], none, g["L3_cond_g2"], none)]
    for l, vs in enumerate(norms):
        for c, v in zip((V_G1, V_BE1, V_G2, V_BE2), vs):
            put(l, c, v)
    for l, bq in ((2, g["L2_cond_bqkv"]), (3, g["L3_cond_b_qkv"])):
        for c, v in zip((V_BQ, V_BK, V_BV), bq.reshape(3, D)):
            put(l, c, v)
    put(3, V_BQR, g["L3_cond_b_qkv"][0:D][swap])
    put(3, V_BKR, g["L3_cond_b_qkv"][D:2 * D][swap])
    for l, v in enumerate((g["L0_cond_b1"], g["L1_cond_b1"], g["L2_cond_b1"], g["L3_cond_b_fc"])):
        put(l, V_B1, v)
    put(3, V_T1, g["L3_cond_b_t1"])
    d["vec"] = vec
    outs = [(none, g["L0_cond_b2"]), (g["L1_cond_bproj"], g["L1_cond_b2"]), (g["L2_cond_bproj"], g["L2_cond_b2"])]
    d["rows"] = np.stack([np.stack([mod[l][2 * D:3 * D], outs[l][0], mod[l][5 * D:6 * D], outs[l][1]]) for l in range(3)])
    d["rows_last"] = np.stack([np.stack([v, v]) for v in (g["L3_cond_b_ao"], g["L3_cond_b_fo"])])

    d["ident"] = np.eye(P, dtype=np.float32)
    d["ident_b"] = np.eye(P, dtype=np.dtype("bfloat16"))
    freq = np.float32(1.0) / np.float32(10000.0) ** (np.arange(0, HD, 2, dtype=np.float32) / np.float32(HD))
    ang = (np.arange(T, dtype=np.float32)[:, None] * freq[None, :]).astype(np.float32)
    f = np.arange(P) % HD
    sign = np.where(f % 2 == 0, -1.0, 1.0).astype(np.float32)
    d["rot"] = np.stack([np.cos(ang).T[f // 2], np.sin(ang).T[f // 2] * sign[:, None]], axis=1).astype(np.float32)
    row, col = np.arange(P)[:, None], np.arange(T)[None, :]
    mask = np.zeros((P, 2, 2, T), np.float32)
    for i in range(2):
        mask[:, 0, i] = np.where(col > i * P + row, MASKED, 0.0)
        mask[:, 1, i] = np.where(i * P + row > col, MASKED, 0.0)
    d["mask"] = mask.astype(np.dtype("bfloat16"))
    return {k: np.ascontiguousarray(v) for k, v in d.items()}


def kernel(**inputs):
    import concourse.bacc as bacc
    from concourse.bass_utils import run_bass_kernel_spmd

    nc = bacc.Bacc("TRN2", target_bir_lowering=False, num_devices=1)
    arrays = {f"in_{k}": v for k, v in lay_out(inputs).items()}
    aps = {k[3:]: nc.dram_tensor(k, v.shape, mybir.dt.from_np(v.dtype), kind="ExternalInput").ap() for k, v in arrays.items()}
    out = nc.dram_tensor("out", (NSEQ, T, D), F32, kind="ExternalOutput").ap()
    build(nc, aps, out)
    return run_bass_kernel_spmd(nc, [arrays], core_ids=[0]).results[0]["out"]
```

```python
import numpy as np
import concourse.bass as bass
from concourse import mybir
from contextlib import ExitStack

F32 = mybir.dt.float32
F32R = mybir.dt.float32r
BF16 = mybir.dt.bfloat16
ALU = mybir.AluOpType
ACT = mybir.ActivationFunctionType
AX = mybir.AxisListType

P = 128
NL = 4
NSEQ = 16
T = 256
D = 256
H = 16
HD = D // H
DFF = 1024
NT = T // P
KD = D // P
NJ = DFF // P
HB = H // 2
STK = 48
ROWS = 64
RING = 4
STACKED = 16 * 4
SCRATCHED = 16 * 6
PRING = 8
NTILE = NL * NSEQ
SCALE = HD ** -0.5
MASKED = -1.0e30
EPS = (1e-5, 1e-5, 1e-5, float(np.finfo(np.float32).eps))
CAUSAL, ROPE = 1, 3
QKV_BIAS = (False, False, True, True)
WQ_COLS = (3 * D, 3 * D, 3 * D, 5 * D)
W1_COLS = (DFF, DFF, DFF, 2 * DFF)
V_SC1, V_SH1, V_SC2, V_SH2, V_G1, V_BE1, V_G2, V_BE2, V_BQ, V_BK, V_BV, V_BQR, V_BKR = range(0, 26, 2)
V_B1 = 26
V_T1 = 42
NVEC = 46
C_S1, C_B1, C_S2, C_B2 = 0, 2, 4, 6
H2T_AT = 8
CHUNK = 1024


def build(nc, a, out):
    ctx = ExitStack()
    with ctx:
        def sb(name, shape, dt=F32):
            return ctx.enter_context(nc.sbuf_tensor(name, shape, dt))

        def sem(name):
            return ctx.enter_context(nc.semaphore(name))

        X = sb("X", [P, NSEQ, NT, D])
        IDENT = sb("IDENT", [P, P])
        IDENTB = sb("IDENTB", [P, P], BF16)
        MASK = sb("MASK", [P, 2, 2, T], BF16)
        ROT = sb("ROT", [P, 2, T])
        VEC = sb("VEC", [P, NL, NVEC])
        COND = sb("COND", [P, NL, 8, NSEQ])
        HALF = sb("HALF", [P, NT])
        WQ = [[sb(f"WQ{p}{x}", [P, KD, max(WQ_COLS[p::2])], F32R) for x in "hl"] for p in range(2)]
        WO = [sb(f"WO{x}", [P, KD, D], F32R) for x in "hl"]
        RAW = [sb(f"RAW{i}", [P, CHUNK // 2]) for i in range(2)]
        XQ = sb("XQ", [P, NT, D])
        TOK = sb("TOK", [P, NT, D])
        ST1, ST2 = sb("ST1", [P, NT, 6]), sb("ST2", [P, NT, 6])
        MV1, MV2 = sb("MV1", [P, NT, 2]), sb("MV2", [P, NT, 2])
        RS1, RS2 = sb("RS1", [P, NT]), sb("RS2", [P, NT])
        TV = sb("TV", [P, NT])
        HF = sb("HF", [P, KD, T])
        H1 = [sb(f"H1{x}", [P, KD, T], F32R) for x in "hl"]
        H2 = [sb(f"H2{x}", [P, KD, T], F32R) for x in "hl"]
        QHL = sb("QHL", [P, 2, KD, T], F32R)
        KHL = sb("KHL", [P, 2, KD, T], F32R)
        QS = sb("QS", [P, HB, T], F32R)
        KS = sb("KS", [P, HB, T], F32R)
        V = sb("V", [P, NT, H, 32])
        NEGM = sb("NEGM", [P, NT, H])
        MT = sb("MT", [H, T], F32R)
        PR = sb("PR", [P, PRING, NT, T])
        OR = sb("OR", [P, 4, T])
        RZ = sb("RZ", [P, NT, H])
        G = sb("G", [P, RING, T])
        GH = [sb(f"GH{x}", [P, RING, T], F32R) for x in "hl"]
        GA = sb("GA", [P, 2, D])
        GM = sb("GM", [P, 2, D])
        B = ctx.enter_context(nc.psum_tensor("B", [P, 8, 512], F32))

        def bank(n, parts=2):
            return B[:, n, :].rearrange("p (a b) -> p a b", a=parts)

        sp_x, sp_const, sp_cw, sp_gs = sem("sp_x"), sem("sp_const"), sem("sp_cw"), sem("sp_gs")
        sp_raw = [sem("sp_raw0"), sem("sp_raw1")]
        sp_ga, sp_gm, sp_scr, sp_stk, sp_mt, sp_out = (sem("sp_" + x) for x in ("ga", "gm", "scr", "stk", "mt", "out"))
        pe_h1, pe_q, pe_k, pe_v, pe_s, pe_mt, pe_st, pe_pv, pe_ot1, pe_ot2, pe_wo, pe_h2, pe_up, pe_dn = (
            sem("pe_" + x) for x in ("h1", "q", "k", "v", "s", "mt", "st", "pv", "ot1", "ot2", "wo", "h2", "up", "dn"))
        ac_h1, ac_v, ac_mt, ac_exp, ac_o, ac_ot, ac_h2, ac_g, ac_w = (
            sem("ac_" + x) for x in ("h1", "v", "mt", "exp", "o", "ot", "h2", "g", "w"))
        dv_st1, dv_mv1, dv_xn1, dv_st2, dv_mv2, dv_xn2, dv_h1, dv_h2, dv_qh, dv_q, dv_kh, dv_k = (
            sem("dv_" + x) for x in ("st1", "mv1", "xn1", "st2", "mv2", "xn2", "h1", "h2", "qh", "q", "kh", "k"))
        dv_max, dv_rz, dv_on, dv_ot, dv_wo, dv_dn, dv_gh, dv_g, dv_rot, dv_rot2 = (
            sem("dv_" + x) for x in ("max", "rz", "on", "ot", "wo", "dn", "gh", "g", "rot", "rot2"))
        po_t1, po_rs1, po_t2, po_rs2, po_h1, po_h2, po_gl, po_xb1, po_x1, po_xb2, po_x2, po_w, po_init = (
            sem("po_" + x) for x in ("t1", "rs1", "t2", "rs2", "h1", "h2", "gl", "xb1", "x1", "xb2", "x2", "w", "init"))
        pc, cc, vc = sem("pe_cond"), sem("ac_cond"), sem("dv_cond")
        dv_init = sem("dv_init")

        q_scr = nc.dram_tensor("q_scratch", [3, HD, HB, KD, T], F32, kind="Internal").ap()
        k_scr = nc.dram_tensor("k_scratch", [3, HD, HB, KD, T], F32, kind="Internal").ap()
        g_scr = nc.dram_tensor("gate_scratch", [NL - 1, NSEQ, 4, D], F32, kind="Internal").ap()

        with ExitStack() as early:
            def esb(name, shape, dt=F32):
                return early.enter_context(nc.sbuf_tensor(name, shape, dt))

            CW = [esb(f"CW{l}", [P, KD, 6 * D]) for l in range(3)]
            CT1 = X[:, 8:10, :, :].rearrange("p s t d -> p s (t d)")
            CT2 = X[:, 10:14, :, :].rearrange("p (k s) t d -> p k (s t d)", k=KD)
            CT = esb("CT", [P, KD, NSEQ])
            SC = esb("SC", [P, KD, NSEQ])
            SLU = esb("SLU", [P, KD, NSEQ])
            Z3 = esb("Z3", [P, KD, NSEQ])
            U = esb("U", [P, 2, NSEQ])
            U2 = esb("U2", [P, 2, NSEQ])
            flat = PR[:].rearrange("p a b c -> p (a b c)")
            GR = flat[0:NSEQ, 0:12 * D].rearrange("p (l r d) -> p l r d", l=NL - 1, r=4)
            RB = [flat[0:NSEQ, 12 * D:16 * D].rearrange("p (r d) -> p r d", r=4), OR[0:NSEQ], G[0:NSEQ]]
            block = early.enter_context(nc.Block())
            ctile = bank(0, 32)
            t1tile = bank(1, 32)
            starts = [(D, 0, 4 * D, 3 * D)] * 3 + [(D, 0, 3 * D, 2 * D)]

            @block.sync
            def _(sp):
                sp.dma_start(CT[:], a["c_t"]).then_inc(sp_cw, 16)
                for l in range(3):
                    sp.dma_start(CW[l][:], a[f"cw{l}"].rearrange("(k p) n -> p k n", p=P)).then_inc(sp_cw, 16)
                sp.dma_start(CT1, a["cw_t1"].rearrange("(k p) n -> p k n", p=P)).then_inc(sp_cw, 16)
                sp.dma_start(CT2, a["cw_t2"].rearrange("(k p) n -> p k n", p=P)).then_inc(sp_cw, 16)
                sp.dma_start(VEC[:], a["vec"]).then_inc(sp_cw, 16)
                for l in range(3):
                    sp.dma_start(RB[l], a["rows"][l].partition_broadcast(NSEQ)).then_inc(sp_cw, 16)
                sp.dma_start(IDENT[:], a["ident"]).then_inc(sp_const, 16)
                sp.dma_start(ROT[:], a["rot"]).then_inc(sp_const, 16)
                sp.dma_start(MASK[:], a["mask"]).then_inc(sp_const, 16)
                sp.dma_start(IDENTB[:], a["ident_b"]).then_inc(sp_const, 16)
                x_in = a["x"].rearrange("s (t p) d -> p s t d", p=P)
                sp.dma_start(X[:, 0:8], x_in[:, 0:8]).then_inc(sp_x, 16)
                sp.wait_ge(vc, 10)
                sp.dma_start(g_scr.rearrange("l s r d -> s l r d"), GR).then_inc(sp_gs, 16)
                sp.wait_ge(pc, 5)
                sp.dma_start(X[:, 8:16], x_in[:, 8:16]).then_inc(sp_x, 16)
                sp.wait_ge(sp_gs, 16)
                sp.wait_ge(sp_x, 32)
                sp.wait_ge(sp_const, 64)

            @block.gpsimd
            def _(po):
                nc.gpsimd.memset(HALF[:], -0.5).then_inc(po_init, 1)
                nc.gpsimd.memset(QS[:].bitcast(F32), 0.0).then_inc(po_init, 1)
                nc.gpsimd.memset(KS[:].bitcast(F32), 1.0).then_inc(po_init, 1)
                nc.gpsimd.memset(V[:], 0.0).then_inc(po_init, 1)
                po.wait_ge(po_init, 4)
                nc.gpsimd.memset(V[:, :, :, HD:HD + 1], 1.0).then_inc(po_init, 1)
                po.wait_ge(po_init, 5)

            @block.scalar
            def _(ac):
                ac.wait_ge(sp_cw, 10 * 16)
                nc.scalar.activation(SC[:], CT[:], ACT.Silu).then_inc(cc, 1)
                ac.wait_ge(pc, 1)
                for k in range(KD):
                    nc.scalar.activation(SLU[:, k, :], t1tile[:, KD + k, :], ACT.Silu,
                                         bias=VEC[:, ROPE, V_T1 + KD + k:V_T1 + KD + k + 1]).then_inc(cc, 1)

            @block.tensor
            def _(pe):
                pe.wait_ge(sp_cw, 10 * 16)
                for f in range(2 * KD):
                    for k in range(KD):
                        last = nc.tensor.matmul(t1tile[:, f, :], CT1[:, k, f * P:(f + 1) * P], CT[:, k, :],
                                                start=(k == 0), stop=(k == KD - 1))
                last.then_inc(pc, 1)
                pe.wait_ge(cc, 1)
                for l in range(3):
                    for r, c0 in enumerate((2 * D, 5 * D)):
                        for k in range(KD):
                            last = nc.tensor.matmul(bank(2 + l)[0:NSEQ, r, :], SC[:, k, :], CW[l][:, k, c0:c0 + D],
                                                    start=(k == 0), stop=(k == KD - 1))
                    last.then_inc(pc, 1)
                for l in range(NL):
                    if l == ROPE:
                        pe.wait_ge(vc, 4)
                    w, m = (CT2, Z3) if l == ROPE else (CW[l], SC)
                    for c, c0 in enumerate(starts[l]):
                        for f in range(KD):
                            for k in range(KD):
                                last = nc.tensor.matmul(ctile[:, 8 * l + 2 * c + f, :],
                                                        w[:, k, c0 + f * P:c0 + (f + 1) * P], m[:, k, :],
                                                        start=(k == 0), stop=(k == KD - 1))
                last.then_inc(pc, 1)

            @block.vector
            def _(dv):
                n = [0]

                def chain(ins):
                    n[0] += 1
                    ins.then_inc(dv_init, 1)

                def settle():
                    dv.wait_ge(dv_init, n[0])

                dv.wait_ge(sp_cw, 10 * 16)
                dv.wait_ge(cc, 3)
                for k in range(KD):
                    nc.vector.scalar_tensor_tensor(Z3[:, k, :], t1tile[:, k, :], VEC[:, ROPE, V_T1 + k:V_T1 + k + 1],
                                                   SLU[:, k, :], ALU.add, ALU.mult).then_inc(vc, 2)
                for l in range(3):
                    dv.wait_ge(pc, 2 + l)
                    for r in range(2):
                        chain(nc.vector.tensor_tensor(GR[:, l, 2 * r, :], bank(2 + l)[0:NSEQ, r, :],
                                                      RB[l][:, 2 * r, :], ALU.add))
                settle()
                for l in range(3):
                    for r in range(2):
                        nc.vector.tensor_tensor(GR[:, l, 2 * r + 1, :], GR[:, l, 2 * r, :], RB[l][:, 2 * r + 1, :],
                                                ALU.mult).then_inc(vc, 1)
                dv.wait_ge(pc, 5)
                for l in range(NL):
                    for half, (sc, sh, g, be, cs, cb) in enumerate(((V_SC1, V_SH1, V_G1, V_BE1, C_S1, C_B1),
                                                                   (V_SC2, V_SH2, V_G2, V_BE2, C_S2, C_B2))):
                        for f in range(KD):
                            def vec(c):
                                return VEC[:, l, c + f:c + f + 1]
                            tile = 8 * l + 4 * half + f
                            chain(nc.vector.tensor_scalar(U[:, f, :], ctile[:, tile, :], vec(sc), 1.0, ALU.add, ALU.add))
                            chain(nc.vector.tensor_scalar(U2[:, f, :], ctile[:, tile + KD, :], vec(sh), None, ALU.add))
                            settle()
                            chain(nc.vector.tensor_scalar(COND[:, l, cs + f, :], U[:, f, :], vec(g), None, ALU.mult))
                            chain(nc.vector.scalar_tensor_tensor(COND[:, l, cb + f, :], U[:, f, :], vec(be), U2[:, f, :],
                                                                 ALU.mult, ALU.add))
                            settle()

        W1 = [sb(f"W1{x}", [P, KD, 2 * DFF], F32R) for x in "hl"]
        W2 = [sb(f"W2{x}", [P, NJ, D], F32R) for x in "hl"]

        HC = CHUNK // 2

        def chunks(l, what):
            if what == "q":
                v = a[f"wq{l}"].rearrange("(k p) n -> p k n", p=P)
                n = WQ_COLS[l]
                dst = WQ[l % 2]
            elif what == "o":
                v, n, dst = a[f"wo{l}"].rearrange("(k p) n -> p k n", p=P), D, WO
            elif what == "1":
                v, n, dst = a[f"w1{l}"].rearrange("(k p) n -> p k n", p=P), W1_COLS[l], W1
            else:
                v = a[f"w2{l}"].rearrange("(j p) n -> p j n", p=P)
                return [(v[:, j:j + 2, :], [w[:, j:j + 2, :] for w in W2], 2) for j in range(0, NJ, 2)]
            if what == "o":
                return [(v, [w[:] for w in dst], 2)]
            step = HC if n % HC == 0 else D
            return [(v[:, k, c:c + step], [w[:, k, c:c + step] for w in dst], 1)
                    for k in range(KD) for c in range(0, n, step)]

        order = []
        first = {}
        done = {}
        for l in range(NL):
            for what in "qo12":
                first[l, what] = len(order)
                order += chunks(l, what)
                done[l, what] = len(order)

        def raw_view(n):
            src, dst, parts = order[n]
            w = dst[0].free_size()
            v = RAW[n % 2][:, 0:w]
            return v.rearrange("p (a b) -> p a b", a=2) if parts == 2 else v

        class Step:

            def __init__(self, t, layer):
                fixed = isinstance(t, int)
                self.first = fixed and t == -2

                def stage(tile):
                    there = not fixed or 0 <= tile < NTILE
                    l = tile // NSEQ if fixed else layer
                    before = max(0, min(tile, NTILE)) if fixed else tile
                    return tile if there else None, l, tile - NSEQ * l, before, before + there

                self.n, self.ln, self.sn, self.nn, self.n_done = stage(t + 2)
                self.q, self.lq, self.sq, self.nq, self.q_done = stage(t + 1)
                self.a, self.la, self.sa, self.na, self.a_done = stage(t)
                self.r, self.lr, self.sr, self.nr, self.r_done = stage(t - 1)
                self.m, self.lm, self.sm, self.nm, self.m_done = stage(t - 2)
                self.conv_q = self.conv_o = self.conv_12 = None
                if fixed:
                    if self.first:
                        self.conv_q = self.conv_o = 0
                    elif t == -1:
                        self.conv_12 = 0
                    elif t % NSEQ == NSEQ - 2 and t < NTILE - 2:
                        self.conv_q = t // NSEQ + 1
                    elif t % NSEQ == 0 and 0 < t < NTILE:
                        self.conv_o = t // NSEQ
                    elif t % NSEQ == 1 and 1 < t < NTILE:
                        self.conv_12 = t // NSEQ

        def seq(s):
            return slice(s, s + 1) if isinstance(s, int) else bass.ds(s, 1)

        def at_least(eng, s, value):
            if not isinstance(value, int) or value > 0:
                eng.wait_ge(s, value)

        def apart(eng):
            eng.nop(nofuse=True)

        def steps(eng, body):
            t = -2
            for l in range(NL):
                lo = NSEQ * l + 2 + (l in (0, ROPE))
                hi = NSEQ * l + NSEQ - 2
                while t < lo:
                    body(Step(t, None))
                    t += 1
                with eng.Fori(lo, hi) as i:
                    body(Step(i, l))
                t = hi
            while t < NTILE + 2:
                body(Step(t, None))
                t += 1

        block = ctx.enter_context(nc.Block())

        @block.tensor
        def _(pe):
            def product(dst, w, x, first_k, last_k):
                for n, (i, j) in enumerate(((0, 0), (0, 1), (1, 0))):
                    last = nc.tensor.matmul(dst, w[i], x[j], start=(first_k and n == 0), stop=(last_k and n == 2))
                return last

            def project(dst, w, x):
                for k in range(KD):
                    last = product(dst, [v[:, k] for v in w], [v[:, k] for v in x], k == 0, k == KD - 1)
                return last

            def cols(w, c):
                return [v[:, :, c:c + P] for v in w]

            def weights(l, what):
                pe.wait_ge(ac_w, done[l, what])
                pe.wait_ge(po_w, done[l, what])

            def body(s):
                def scores(h):
                    a_, b = s.a, ROWS * (h // HB)
                    if h == 0:
                        pe.wait_ge(sp_stk, STACKED * (a_ + 1))
                        at_least(pe, ac_exp, H * s.na)
                    elif h >= 2:
                        pe.wait_ge(dv_max, H * a_ + h - 1)
                    for i in range(NT):
                        dst = bank(4 + h % 2)[:, i, :]
                        last = nc.tensor.matmul(dst, QS[b:b + STK, h % HB, i * P:(i + 1) * P], KS[b:b + STK, h % HB, :],
                                                start=True, stop=(s.la != CAUSAL))
                        if s.la == CAUSAL:
                            last = nc.tensor.matmul(dst, IDENTB[:], MASK[:, 0, i, :], start=False, stop=True)
                    last.then_inc(pe_s, 1)

                def up(j):
                    m, dst = s.m, bank(3 - j % 2)
                    if j == 0:
                        weights(s.lm, "1")
                        pe.wait_ge(dv_h2, m + 1)
                        pe.wait_ge(po_h2, m + 1)
                        at_least(pe, dv_k, s.nq)
                    elif j == 1:
                        at_least(pe, dv_k, s.nq)
                        at_least(pe, ac_v, s.nq)
                    elif s.lm == ROPE:
                        pe.wait_ge(dv_g, NJ * (m - NSEQ * ROPE) + j - 1)
                    else:
                        pe.wait_ge(ac_g, NJ * m + j - 1)
                    last = project(dst[:, 0, :], cols(W1, j * P), H2)
                    if s.lm == ROPE:
                        last = project(dst[:, 1, :], cols(W1, DFF + j * P), H2)
                    last.then_inc(pe_up, 1)

                def down(j):
                    m = s.m
                    if j == 0:
                        weights(s.lm, "2")
                        at_least(pe, dv_wo, s.r_done)
                        at_least(pe, ac_o, 2 * s.na)
                    pe.wait_ge(dv_gh, NJ * m + j + 1)
                    pe.wait_ge(po_gl, NJ * m + j + 1)
                    for i in range(NT):
                        for n, (x, y) in enumerate(((0, 0), (0, 1), (1, 0))):
                            last = nc.tensor.matmul(bank(7)[:, i, :], GH[x][:, j % RING, i * P:(i + 1) * P],
                                                    W2[y][:, j, :], start=(j == 0 and n == 0 and i == 0),
                                                    stop=(j == NJ - 1 and n == 2), skip_group_check=True)
                    last.then_inc(pe_dn, 1)

                def to_features(dst, src):
                    for f in range(KD):
                        for i in range(NT):
                            last = nc.tensor.transpose(dst[:, f, i * P:(i + 1) * P], src[:, i, f * P:(f + 1) * P], IDENT[:])
                    return last

                def outputs_to_tokens():
                    pe.wait_ge(ac_o, 2 * s.r + 2)
                    at_least(pe, ac_h2, s.nr)
                    at_least(pe, dv_q, s.nq)
                    for i in range(NT):
                        for g in range(4):
                            last = nc.tensor.transpose(bank(i, 4)[:, g, :], OR[:, g, i * P:(i + 1) * P], IDENT[:])
                        last.then_inc(pe_ot1, 1)

                def outputs_to_features():
                    pe.wait_ge(dv_on, 2 * s.r + 2)
                    to_features(bank(6), TOK).then_inc(pe_ot2, 1)

                def output_projection():
                    weights(s.lr, "o")
                    pe.wait_ge(ac_ot, s.r + 1)
                    pe.wait_ge(dv_ot, s.r + 1)
                    for i in range(NT):
                        for k in range(KD):
                            last = product(bank(7)[:, i, :], [x[:, k, i * P:(i + 1) * P] for x in H1],
                                           [w[:, k, :] for w in WO], k == 0, k == KD - 1)
                    last.then_inc(pe_wo, 1)

                def norm_1():
                    pe.wait_ge(dv_xn1, s.q + 1)
                    at_least(pe, dv_q, s.nq)
                    at_least(pe, dv_on, 2 * s.r_done)
                    to_features(bank(1), XQ).then_inc(pe_h1, 1)

                def norm_2():
                    pe.wait_ge(dv_xn2, s.r + 1)
                    to_features(bank(0), TOK).then_inc(pe_h2, 1)

                for j in range(NJ):
                    if s.r is not None:
                        if j == 1:
                            outputs_to_tokens()
                        if j == 3:
                            outputs_to_features()
                        if j == 5:
                            output_projection()
                    if j == 6 and s.q is not None:
                        norm_1()
                    if s.m is not None:
                        up(j)
                        if j >= 6:
                            down(j - 6)
                for h in range(H):
                    if s.a is not None:
                        scores(h)
                    if h % 2 == 1 and h // 2 + 2 < NJ and s.m is not None:
                        down(h // 2 + 2)
                    if h == H2T_AT and s.r is not None:
                        norm_2()
                if s.q is not None:
                    wq, rope = WQ[s.lq % 2], s.lq == ROPE
                    weights(s.lq, "q")
                    pe.wait_ge(dv_h1, s.q + 1)
                    pe.wait_ge(po_h1, s.q + 1)
                    for f in range(KD):
                        last = project(bank(1)[:, f, :], cols(wq, f * P), H1)
                    if rope:
                        at_least(pe, ac_h2, s.r_done)
                        for f in range(KD):
                            last = project(bank(0)[:, f, :], cols(wq, 3 * D + f * P), H1)
                    last.then_inc(pe_q, 1)
                if s.a is not None:
                    pe.wait_ge(dv_max, H * s.a + H)
                    at_least(pe, ac_ot, s.r_done)
                    at_least(pe, dv_ot, s.r_done)
                    for i in range(NT):
                        last = nc.tensor.transpose(B[0:H, 6, i * P:(i + 1) * P], NEGM[:, i, :], IDENT[:])
                    last.then_inc(pe_mt, 1)
                if s.q is not None:
                    if s.m is not None:
                        if s.lm == ROPE:
                            pe.wait_ge(dv_g, NJ * (s.m - NSEQ * ROPE) + NJ)
                        else:
                            pe.wait_ge(ac_g, NJ * s.m + NJ)
                    at_least(pe, ac_v, s.nq)
                    at_least(pe, dv_k, s.nq)
                    for f in range(KD):
                        last = project(bank(3)[:, f, :], cols(wq, D + f * P), H1)
                    if rope:
                        for f in range(KD):
                            last = project(bank(2)[:, f, :], cols(wq, 4 * D + f * P), H1)
                    last.then_inc(pe_k, 1)

                def values():
                    if rope:
                        pe.wait_ge(dv_k, s.q + 1)
                    for i in range(NT):
                        for k in range(KD):
                            last = product(bank(2)[:, i, :], [x[:, k, i * P:(i + 1) * P] for x in H1],
                                           [w[:, k, 2 * D:3 * D] for w in wq], k == 0, k == KD - 1)
                    last.then_inc(pe_v, 1)

                if s.q is not None and (s.a is None or not rope):
                    values()

                if s.a is not None:
                    a_ = s.a

                    def outputs(g):
                        pe.wait_ge(ac_exp, H * a_ + 4 * g + 4)
                        if g == 0:
                            pe.wait_ge(ac_v, a_ + 1)
                            pe.wait_ge(ac_mt, a_ + 1)
                        if g == 2:
                            at_least(pe, dv_dn, s.m_done)
                        for k in range(NT):
                            for j in range(4):
                                h = 4 * g + j
                                last = nc.tensor.matmul(bank(6 + g // 2)[32 * j:32 * j + 32, g % 2, :],
                                                        V[:, k, h, :], PR[:, h % PRING, k, :],
                                                        start=(k == 0), stop=(k == NT - 1))
                        last.then_inc(pe_pv, 1)

                    pe.wait_ge(sp_mt, 32 * (a_ + 1))
                    for h in range(H):
                        b = ROWS * (h // HB)
                        if h >= 2:
                            pe.wait_ge(ac_exp, H * a_ + h - 1)
                        for k in range(NT):
                            dst = bank(4 + h % 2)[:, k, :]
                            last = nc.tensor.matmul(dst, KS[b:b + ROWS, h % HB, k * P:(k + 1) * P],
                                                    QS[b:b + ROWS, h % HB, :], start=True, stop=(s.la != CAUSAL))
                            if s.la == CAUSAL:
                                last = nc.tensor.matmul(dst, IDENTB[:], MASK[:, 1, k, :], start=False, stop=True)
                        last.then_inc(pe_st, 1)
                        if h % 4 == 2 and h > 4:
                            outputs(h // 4 - 1)
                        if h == HB and s.q is not None and rope:
                            values()
                    outputs(3)
            steps(pe, body)

        @block.scalar
        def _(ac):
            def split_hi(l, what):
                for n in range(first[l, what], done[l, what]):
                    ac.wait_ge(sp_raw[n % 2], 16 * (n // 2 + 1))
                    nc.scalar.activation(order[n][1][0], raw_view(n), ACT.Copy).then_inc(ac_w, 1)

            def cond(s, layer, sequence, c):
                return COND[:, layer, c, seq(sequence)]

            def body(s):
                if s.m is None:
                    if s.r is not None:
                        outputs_hi(s)
                    modulate(s, s.q, s.lq, s.sq, 0)
                for j in range(NJ) if s.m is not None else ():
                    m = s.m
                    ac.wait_ge(pe_up, NJ * m + j + 1)
                    if j == 0:
                        at_least(ac, dv_k, s.nq)
                    at_least(ac, dv_gh, NJ * m + j + 1 - RING)
                    at_least(ac, po_gl, NJ * m + j + 1 - RING)
                    if s.lm == ROPE:
                        nc.scalar.activation(G[:, j % RING, :], bank(3 - j % 2)[:, 1, :], ACT.Silu,
                                             bias=VEC[:, ROPE, V_B1 + NJ + j:V_B1 + NJ + j + 1]).then_inc(ac_g, 1)
                    else:
                        nc.scalar.activation(G[:, j % RING, :], bank(3 - j % 2)[:, 0, :], ACT.Gelu,
                                             bias=VEC[:, s.lm, V_B1 + j:V_B1 + j + 1]).then_inc(ac_g, 1)
                    if j == 2 and s.r is not None:
                        outputs_hi(s)
                    if j == 5:
                        modulate(s, s.q, s.lq, s.sq, 0)
                modulate(s, s.r, s.lr, s.sr, 1)
                if s.a is not None:
                    a_ = s.a
                    ac.wait_ge(pe_mt, a_ + 1)
                    at_least(ac, sp_mt, 32 * s.na)
                    nc.scalar.activation(MT[:], B[0:H, 6, 0:T], ACT.Copy).then_inc(ac_mt, 1)
                    for h in range(H):
                        ac.wait_ge(pe_st, H * a_ + h + 1)
                        at_least(ac, pe_pv, 4 * a_ + h // 4 - 1)
                        nc.scalar.activation(PR[:, h % PRING, :, :], bank(4 + h % 2), ACT.Exp, scale=SCALE).then_inc(ac_exp, 1)
                        if h == 12:
                            evacuate(s, 0)
                    evacuate(s, 1)
                if s.q is not None:
                    ac.wait_ge(pe_v, s.q + 1)
                    at_least(ac, pe_pv, 4 * s.a_done)
                    nc.scalar.activation(V[:, :, :, 0:HD], B[:, 2, :].rearrange("p (i h d) -> p i h d", i=NT, h=H),
                                         ACT.Copy).then_inc(ac_v, 1)
                if s.conv_q is not None:
                    split_hi(s.conv_q, "q")
                if s.conv_o is not None:
                    split_hi(s.conv_o, "o")
                if s.conv_12 is not None:
                    split_hi(s.conv_12, "1")
                    split_hi(s.conv_12, "2")

            def outputs_hi(s):
                ac.wait_ge(pe_ot2, s.r + 1)
                at_least(ac, pe_v, s.nq)
                for f in range(KD):
                    if QKV_BIAS[s.lr]:
                        last = nc.scalar.activation(H1[0][:, f, :], bank(6)[:, f, :], ACT.Identity,
                                                    bias=VEC[:, s.lr, V_BV + f:V_BV + f + 1])
                    else:
                        last = nc.scalar.activation(H1[0][:, f, :], bank(6)[:, f, :], ACT.Copy)
                last.then_inc(ac_ot, 1)

            def evacuate(s, half):
                ac.wait_ge(pe_pv, 4 * s.a + 2 * half + 2)
                at_least(ac, pe_ot1, 2 * s.r_done)
                nc.scalar.activation(OR[:, 2 * half:2 * half + 2, :], bank(6 + half), ACT.Copy).then_inc(ac_o, 1)

            def modulate(s, tile, layer, sequence, second):
                if tile is None:
                    return
                if second:
                    nbank, sc, sh, s_pe, s_ac = 0, C_S2, C_B2, pe_h2, ac_h2
                    at_least(ac, dv_h1, s.q_done)
                    at_least(ac, po_h1, s.q_done)
                else:
                    nbank, sc, sh, s_pe, s_ac = 1, C_S1, C_B1, pe_h1, ac_h1
                    at_least(ac, dv_h2, s.nr)
                    at_least(ac, po_h2, s.nr)
                ac.wait_ge(s_pe, tile + 1)
                for f in range(KD):
                    last = nc.scalar.activation(HF[:, f, :], bank(nbank)[:, f, :], ACT.Identity,
                                                bias=cond(s, layer, sequence, sh + f), scale=cond(s, layer, sequence, sc + f))
                last.then_inc(s_ac, 1)

            steps(ac, body)

        @block.vector
        def _(dv):
            def statistics(x, st, mv, s_st, s_mv, n):
                for i in range(NT):
                    last = nc.vector.bn_stats(st[:, i, :], x[i])
                last.then_inc(s_st, 1)
                dv.wait_ge(s_st, n + 1)
                apart(dv)
                for i in range(NT):
                    last = nc.vector.bn_aggr(mv[:, i, :], st[:, i, :])
                last.then_inc(s_mv, 1)

            def normalise(dst, x, mv, rs, s_xn, rms):
                for i in range(NT):
                    if rms:
                        last = nc.vector.tensor_scalar(dst[:, i, :], x[i], rs[:, i:i + 1], None, ALU.mult)
                    else:
                        last = nc.vector.tensor_scalar(dst[:, i, :], x[i], mv[:, i, 0:1], rs[:, i:i + 1],
                                                       ALU.subtract, ALU.mult)
                last.then_inc(s_xn, 1)

            def tokens(sequence):
                return [X[:, seq(sequence), i, :] for i in range(NT)]

            def body(s):
                def maximum(h):
                    a_ = s.a
                    dv.wait_ge(pe_s, H * a_ + h + 1)
                    if h == 0:
                        at_least(dv, pe_mt, s.na)
                    nc.vector.tensor_reduce(NEGM[:, :, h], bank(4 + h % 2), op=ALU.max, axis=AX.X,
                                            negate=True).then_inc(dv_max, 1)

                def hidden(j):
                    m = s.m
                    dv.wait_ge(ac_g, NJ * m + j + 1)
                    if s.lm == ROPE:
                        nc.vector.scalar_tensor_tensor(G[:, j % RING, :], bank(3 - j % 2)[:, 0, :],
                                                       VEC[:, ROPE, V_B1 + j:V_B1 + j + 1], G[:, j % RING, :],
                                                       ALU.add, ALU.mult).then_inc(dv_g, 1)
                        dv.wait_ge(dv_g, NJ * (m - NSEQ * ROPE) + j + 1)
                    at_least(dv, pe_dn, NJ * m + j + 1 - RING)
                    nc.vector.tensor_copy(GH[0][:, j % RING, :], G[:, j % RING, :]).then_inc(dv_gh, 1)

                def split_1():
                    if s.q is None:
                        return
                    dv.wait_ge(ac_h1, s.q + 1)
                    at_least(dv, pe_v, s.nq)
                    at_least(dv, pe_wo, s.r_done)
                    nc.vector.tensor_copy(H1[0][:], HF[:]).then_inc(dv_h1, 1)

                def normalised_outputs():
                    at_least(dv, po_x2, s.nm)
                    for i in range(NT):
                        dv.wait_ge(pe_ot1, 2 * s.r + i + 1)
                        heads = B[:, i, :].rearrange("p (h c) -> p h c", h=H)
                        nc.vector.reciprocal(RZ[:, i, :], heads[:, :, HD]).then_inc(dv_rz, 1)
                        dv.wait_ge(dv_rz, 2 * s.r + i + 1)
                        nc.vector.tensor_tensor(TOK[:, i, :].rearrange("p (h d) -> p h d", h=H), heads[:, :, 0:HD],
                                                RZ[:, i, :].unsqueeze(2).to_broadcast([P, H, HD]),
                                                ALU.mult).then_inc(dv_on, 1)

                def outputs_lo():
                    dv.wait_ge(ac_ot, s.r + 1)
                    if QKV_BIAS[s.lr]:
                        for f in range(KD):
                            last = nc.vector.scalar_tensor_tensor(H1[1][:, f, :], bank(6)[:, f, :],
                                                                  VEC[:, s.lr, V_BV + f:V_BV + f + 1],
                                                                  H1[0][:, f, :].bitcast(F32), ALU.add, ALU.subtract)
                    else:
                        last = nc.vector.tensor_tensor(H1[1][:], bank(6), H1[0][:].bitcast(F32), ALU.subtract)
                    last.then_inc(dv_ot, 1)

                if s.r is not None:
                    normalised_outputs()
                for j in range(NJ):
                    if s.m is not None and j < 6:
                        hidden(j)
                    if s.r is not None:
                        if j == 0:
                            outputs_lo()
                        if j == 2:
                            dv.wait_ge(pe_wo, s.r + 1)
                            multiply(s, bank(7), GA, sp_ga, s.r, s.lr).then_inc(dv_wo, 1)
                split_1()
                for h in range(H):
                    if s.a is not None:
                        maximum(h)
                    if s.m is not None and h in (0, 1):
                        hidden(6 + h)
                    if s.r is not None:
                        if h == 1:
                            dv.wait_ge(po_x1, s.r + 1)
                            statistics(tokens(s.sr), ST2, MV2, dv_st2, dv_mv2, s.r)
                        if h == 5:
                            dv.wait_ge(po_rs2, s.r + 1)
                            normalise(TOK, tokens(s.sr), MV2, RS2, dv_xn2, s.lr == ROPE)
                        if h == 12:
                            dv.wait_ge(ac_h2, s.r + 1)
                            at_least(dv, pe_up, NJ * s.m_done)
                            nc.vector.tensor_copy(H2[0][:], HF[:]).then_inc(dv_h2, 1)
                if s.m is not None:
                    dv.wait_ge(pe_dn, NJ * s.m + NJ)
                    at_least(dv, pe_h2, s.r_done)
                    multiply(s, bank(7), GM, sp_gm, s.m, s.lm).then_inc(dv_dn, 1)
                if s.q is not None:
                    split_qk(s, pe_q, QHL, 1, 0, V_BQ, V_BQR, dv_qh, dv_q, 0)
                    split_qk(s, pe_k, KHL, 3, 2, V_BK, V_BKR, dv_kh, dv_k, 1)
                if s.n is not None:
                    if s.ln > 0:
                        dv.wait_ge(po_x2, s.n - (NSEQ - 1))
                    statistics(tokens(s.sn), ST1, MV1, dv_st1, dv_mv1, s.n)
                    dv.wait_ge(po_rs1, s.n + 1)
                    at_least(dv, pe_h1, s.q_done)
                    normalise(XQ, tokens(s.sn), MV1, RS1, dv_xn1, s.ln == ROPE)

            def multiply(s, src, rows, s_rows, n, layer):
                if layer == ROPE:
                    return nc.vector.tensor_copy(TOK[:], src)
                dv.wait_ge(s_rows, 16 * (n + 1))
                return nc.vector.tensor_tensor(TOK[:], src, rows[:, 0:1, :].to_broadcast([P, NT, D]), ALU.mult)

            def split_qk(s, s_pe, dst, nbank, nswap, vb, vbr, s_hi, s_lo, which):
                dv.wait_ge(s_pe, s.q + 1)
                at_least(dv, sp_scr, SCRATCHED * s.nq)
                if s.lq == ROPE:
                    if s.m is not None:
                        dv.wait_ge(po_gl, NJ * s.m_done)
                    if which == 1:
                        dv.wait_ge(dv_q, s.q + 1)
                    r = s.q - NSEQ * ROPE
                    for c, nb, b in ((0, nbank, vb), (1, nswap, vbr)):
                        for f in range(KD):
                            last = nc.vector.scalar_tensor_tensor(G[:, 2 * c + f, :], bank(nb)[:, f, :],
                                                                  VEC[:, ROPE, b + f:b + f + 1], ROT[:, c, :],
                                                                  ALU.add, ALU.mult)
                    last.then_inc(dv_rot, 1)
                    dv.wait_ge(dv_rot, 2 * r + which + 1)
                    nc.vector.tensor_tensor(G[:, 0:2, :], G[:, 0:2, :], G[:, 2:4, :], ALU.add).then_inc(dv_rot2, 1)
                    dv.wait_ge(dv_rot2, 2 * r + which + 1)
                    nc.vector.tensor_copy(dst[:, 0], G[:, 0:2, :]).then_inc(s_hi, 1)
                    dv.wait_ge(s_hi, s.q + 1)
                    nc.vector.tensor_tensor(dst[:, 1], G[:, 0:2, :], dst[:, 0].bitcast(F32), ALU.subtract).then_inc(s_lo, 1)
                elif QKV_BIAS[s.lq]:
                    for f in range(KD):
                        last = nc.vector.tensor_scalar(dst[:, 0, f, :], bank(nbank)[:, f, :],
                                                       VEC[:, s.lq, vb + f:vb + f + 1], None, ALU.add)
                    last.then_inc(s_hi, 1)
                    dv.wait_ge(s_hi, s.q + 1)
                    for f in range(KD):
                        last = nc.vector.scalar_tensor_tensor(dst[:, 1, f, :], bank(nbank)[:, f, :],
                                                              VEC[:, s.lq, vb + f:vb + f + 1],
                                                              dst[:, 0, f, :].bitcast(F32), ALU.add, ALU.subtract)
                    last.then_inc(s_lo, 1)
                else:
                    nc.vector.tensor_copy(dst[:, 0], bank(nbank)).then_inc(s_hi, 1)
                    dv.wait_ge(s_hi, s.q + 1)
                    nc.vector.tensor_tensor(dst[:, 1], bank(nbank), dst[:, 0].bitcast(F32), ALU.subtract).then_inc(s_lo, 1)

            steps(dv, body)

        @block.gpsimd
        def _(po):
            def split_lo(l, what):
                for n in range(first[l, what], done[l, what]):
                    po.wait_ge(ac_w, n + 1)
                    nc.gpsimd.tensor_tensor(order[n][1][1], raw_view(n), order[n][1][0].bitcast(F32),
                                            ALU.subtract).then_inc(po_w, 1)

            def rstd(mv, rs, s_mv, s_t, s_rs, n, layer):
                po.wait_ge(s_mv, n + 1)
                if layer == ROPE:
                    nc.gpsimd.tensor_tensor(TV[:], mv[:, :, 0], mv[:, :, 0], ALU.mult).then_inc(s_t, 1)
                    po.wait_ge(s_t, n + 2 * (n - NSEQ * ROPE) + 1)
                    nc.gpsimd.tensor_tensor(TV[:], TV[:], mv[:, :, 1], ALU.add).then_inc(s_t, 1)
                    po.wait_ge(s_t, n + 2 * (n - NSEQ * ROPE) + 2)
                    apart(po)
                    nc.gpsimd.tensor_scalar(TV[:], TV[:], EPS[layer], None, ALU.add).then_inc(s_t, 1)
                    po.wait_ge(s_t, n + 2 * (n - NSEQ * ROPE) + 3)
                else:
                    apart(po)
                    nc.gpsimd.tensor_scalar(TV[:], mv[:, :, 1], EPS[layer], None, ALU.add).then_inc(s_t, 1)
                    po.wait_ge(s_t, n + 1)
                nc.gpsimd.tensor_tensor(rs[:], TV[:], HALF[:], ALU.pow).then_inc(s_rs, 1)

            def bias_rows(layer, n):
                return not (layer == 0 and n == 0)

            def x_of(sequence):
                return X[:, seq(sequence), :, :].rearrange("p a t d -> p (a t) d")

            def residual_1(s):
                x = x_of(s.sr)
                po.wait_ge(dv_xn1, s.r + 1)
                po.wait_ge(sp_ga, 16 * (s.r + 1))
                apart(po)
                nc.gpsimd.tensor_tensor(x, x, GA[:, 1:2, :].to_broadcast([P, NT, D]), ALU.add).then_inc(po_xb1, 1)
                po.wait_ge(po_xb1, s.r + 1)
                po.wait_ge(dv_wo, s.r + 1)
                apart(po)
                nc.gpsimd.tensor_tensor(x, x, TOK[:], ALU.add).then_inc(po_x1, 1)

            def body(s):
                for j in range(NJ):
                    if s.m is not None:
                        po.wait_ge(dv_gh, NJ * s.m + j + 1)
                        nc.gpsimd.tensor_tensor(GH[1][:, j % RING, :], G[:, j % RING, :], GH[0][:, j % RING, :].bitcast(F32),
                                                ALU.subtract).then_inc(po_gl, 1)
                    if j == 2 and s.r is not None:
                        residual_1(s)
                    if j == 5:
                        low_1(s)
                if s.r is not None:
                    rstd(MV2, RS2, dv_mv2, po_t2, po_rs2, s.r, s.lr)
                    po.wait_ge(ac_h2, s.r + 1)
                    po.wait_ge(dv_h2, s.r + 1)
                    nc.gpsimd.tensor_tensor(H2[1][:], HF[:], H2[0][:].bitcast(F32), ALU.subtract).then_inc(po_h2, 1)
                if s.m is not None:
                    m, xm = s.m, x_of(s.sm)
                    po.wait_ge(dv_xn2, m + 1)
                    po.wait_ge(sp_gm, 16 * (m + 1))
                    apart(po)
                    nc.gpsimd.tensor_tensor(xm, xm, GM[:, 1:2, :].to_broadcast([P, NT, D]), ALU.add).then_inc(po_xb2, 1)
                    po.wait_ge(po_xb2, m + 1)
                    po.wait_ge(dv_dn, m + 1)
                    apart(po)
                    nc.gpsimd.tensor_tensor(xm, xm, TOK[:], ALU.add).then_inc(po_x2, 1)
                if s.n is not None:
                    rstd(MV1, RS1, dv_mv1, po_t1, po_rs1, s.n, s.ln)
                if s.conv_q is not None:
                    split_lo(s.conv_q, "q")
                if s.conv_o is not None:
                    split_lo(s.conv_o, "o")
                if s.conv_12 is not None:
                    split_lo(s.conv_12, "1")
                    split_lo(s.conv_12, "2")

            def low_1(s):
                if s.q is None:
                    return
                po.wait_ge(dv_h1, s.q + 1)
                nc.gpsimd.tensor_tensor(H1[1][:], HF[:], H1[0][:].bitcast(F32), ALU.subtract).then_inc(po_h1, 1)

            steps(po, body)

        @block.sync
        def _(sp):
            def hold(s, value):
                at_least(sp, s, value)
                apart(sp)

            def load_raw(l, what):
                for n in range(first[l, what], done[l, what]):
                    if n >= 2:
                        hold(po_w, n - 1)
                    sp.dma_start(raw_view(n), order[n][0]).then_inc(sp_raw[n % 2], 16)

            def rows(dst, layer, sequence, half):
                if layer == ROPE:
                    return dst[:], a["rows_last"][half].partition_broadcast(P)
                src = g_scr[layer, seq(sequence), 2 * half:2 * half + 2, :].rearrange("a r d -> (a r) d")
                return dst[:], src.partition_broadcast(P)

            def store(s, tile, sequence):
                hold(po_x2, tile + 1)
                o = out[seq(sequence), :, :].rearrange("a (t p) d -> p (a t) d", p=P)
                sp.dma_start(o, X[:, seq(sequence), :, :].rearrange("p a t d -> p (a t) d")).then_inc(sp_out, 16)

            def body(s):
                if s.r is not None:
                    hold(dv_wo, s.nr)
                    hold(po_xb1, s.nr)
                    sp.dma_start(*rows(GA, s.lr, s.sr, 0)).then_inc(sp_ga, 16)
                if s.m is not None:
                    hold(dv_dn, s.nm)
                    hold(po_xb2, s.nm)
                    sp.dma_start(*rows(GM, s.lm, s.sm, 1)).then_inc(sp_gm, 16)
                    if s.lm == ROPE and not (isinstance(s.m, int) and s.m == NSEQ * ROPE):
                        store(s, s.m - 1, s.sm - 1)
                if s.a is not None:
                    hold(ac_mt, s.a + 1)
                    for half in range(2):
                        row = ROWS * half + STK
                        sp.dma_start(QS[row:row + 1, :, :].bitcast(F32),
                                     MT[HB * half:HB * half + HB, :].bitcast(F32)).then_inc(sp_mt, 16)
                if s.q is not None:
                    hold(sp_stk, STACKED * s.nq)
                    for s_dv, src, scr, ranks in ((dv_q, QHL, q_scr, (0, 1, 0)), (dv_k, KHL, k_scr, (0, 0, 1))):
                        hold(s_dv, s.q + 1)
                        for r, x in enumerate(ranks):
                            sp.dma_start(scr[r].rearrange("d h f n -> h d (f n)"),
                                         src[:, x].rearrange("p f n -> p (f n)").bitcast(F32)).then_inc(sp_scr, 16)
                    hold(sp_scr, SCRATCHED * (s.q + 1))
                    hold(pe_st, H * s.a_done)
                    for scr, dst in ((q_scr, QS), (k_scr, KS)):
                        for half in range(2):
                            b = ROWS * half
                            sp.dma_start(dst[b:b + STK, :, :].bitcast(F32),
                                         scr[:, :, :, half, :].rearrange("r d h n -> (r d) h n")).then_inc(sp_stk, 16)
                if s.conv_q is not None:
                    load_raw(s.conv_q, "q")
                if s.conv_o is not None:
                    load_raw(s.conv_o, "o")
                if s.conv_12 is not None:
                    load_raw(s.conv_12, "1")
                    load_raw(s.conv_12, "2")

            steps(sp, body)
            store(None, NTILE - 1, NSEQ - 1)
            sp.wait_ge(sp_out, 16 * NSEQ)


def lay_out(i):
    g = {k: np.asarray(v) for k, v in i.items()}
    d = {"x": g["x"]}

    def cols(v):
        return np.asarray(v).reshape(-1, P).T

    d["c_t"] = np.ascontiguousarray(g["cond_1024"].T.reshape(KD, P, NSEQ).transpose(1, 0, 2))
    d["cw0"], d["cw1"], d["cw2"] = g["L0_cond_wc"].T, g["L1_cond_Wada"], g["L2_cond_Wt"]
    d["cw_t1"], d["cw_t2"] = g["L3_cond_w_t1"], g["L3_cond_w_t2"]
    rep = H // 4

    def spread(w):
        return np.repeat(w.T.reshape(D, 4, 1, HD), rep, axis=2).reshape(D, D)

    swap = np.arange(D).reshape(-1, 2)[:, ::-1].reshape(-1)
    w3 = g["L3_cond_w_qkv"]
    d["wq0"] = np.concatenate([g["L0_cond_wq"].T, spread(g["L0_cond_wk"]), spread(g["L0_cond_wv"])], axis=1)
    d["wq1"], d["wq2"] = g["L1_cond_Wqkv"], g["L2_cond_Wqkv"]
    d["wq3"] = np.concatenate([w3, w3[:, 0:D][:, swap], w3[:, D:2 * D][:, swap]], axis=1)
    d["wo0"], d["wo1"], d["wo2"], d["wo3"] = g["L0_cond_wo"].T, g["L1_cond_Wproj"], g["L2_cond_Wproj"], g["L3_cond_w_ao"]
    d["w10"], d["w11"], d["w12"], d["w13"] = g["L0_cond_w1"].T, g["L1_cond_W1"], g["L2_cond_W1"], g["L3_cond_w_fc"]
    d["w20"], d["w21"], d["w22"], d["w23"] = g["L0_cond_w2"].T, g["L1_cond_W2"], g["L2_cond_W2"], g["L3_cond_w_fo"]

    one, none = np.ones(D, np.float32), np.zeros(D, np.float32)
    vec = np.zeros((P, NL, NVEC), np.float32)

    def put(l, c, v):
        v = cols(v)
        vec[:, l, c:c + v.shape[1]] = v

    mod = [g["L0_cond_bc"], g["L1_cond_bada"], g["L2_cond_bt"]]
    for l in range(3):
        b = mod[l].reshape(6, D)
        for c, v in ((V_SH1, b[0]), (V_SC1, b[1]), (V_SH2, b[3]), (V_SC2, b[4])):
            put(l, c, v)
    b = g["L3_cond_b_t2"].reshape(4, D)
    for c, v in ((V_SH1, b[0]), (V_SC1, b[1]), (V_SH2, b[2]), (V_SC2, b[3])):
        put(3, c, v)
    norms = [(one, none, one, none)] + [tuple(g[f"L{l}_cond_{n}"] for n in ("g1", "be1", "g2", "be2")) for l in (1, 2)] + [
        (g["L3_cond_g1"], none, g["L3_cond_g2"], none)]
    for l, vs in enumerate(norms):
        for c, v in zip((V_G1, V_BE1, V_G2, V_BE2), vs):
            put(l, c, v)
    for l, bq in ((2, g["L2_cond_bqkv"]), (3, g["L3_cond_b_qkv"])):
        for c, v in zip((V_BQ, V_BK, V_BV), bq.reshape(3, D)):
            put(l, c, v)
    put(3, V_BQR, g["L3_cond_b_qkv"][0:D][swap])
    put(3, V_BKR, g["L3_cond_b_qkv"][D:2 * D][swap])
    for l, v in enumerate((g["L0_cond_b1"], g["L1_cond_b1"], g["L2_cond_b1"], g["L3_cond_b_fc"])):
        put(l, V_B1, v)
    put(3, V_T1, g["L3_cond_b_t1"])
    d["vec"] = vec
    outs = [(none, g["L0_cond_b2"]), (g["L1_cond_bproj"], g["L1_cond_b2"]), (g["L2_cond_bproj"], g["L2_cond_b2"])]
    d["rows"] = np.stack([np.stack([mod[l][2 * D:3 * D], outs[l][0], mod[l][5 * D:6 * D], outs[l][1]]) for l in range(3)])
    d["rows_last"] = np.stack([np.stack([v, v]) for v in (g["L3_cond_b_ao"], g["L3_cond_b_fo"])])

    d["ident"] = np.eye(P, dtype=np.float32)
    d["ident_b"] = np.eye(P, dtype=np.dtype("bfloat16"))
    freq = np.float32(1.0) / np.float32(10000.0) ** (np.arange(0, HD, 2, dtype=np.float32) / np.float32(HD))
    ang = (np.arange(T, dtype=np.float32)[:, None] * freq[None, :]).astype(np.float32)
    f = np.arange(P) % HD
    sign = np.where(f % 2 == 0, -1.0, 1.0).astype(np.float32)
    d["rot"] = np.stack([np.cos(ang).T[f // 2], np.sin(ang).T[f // 2] * sign[:, None]], axis=1).astype(np.float32)
    row, col = np.arange(P)[:, None], np.arange(T)[None, :]
    mask = np.zeros((P, 2, 2, T), np.float32)
    for i in range(2):
        mask[:, 0, i] = np.where(col > i * P + row, MASKED, 0.0)
        mask[:, 1, i] = np.where(i * P + row > col, MASKED, 0.0)
    d["mask"] = mask.astype(np.dtype("bfloat16"))
    return {k: np.ascontiguousarray(v) for k, v in d.items()}


def kernel(**inputs):
    import concourse.bacc as bacc
    from concourse.bass_utils import run_bass_kernel_spmd

    nc = bacc.Bacc("TRN2", target_bir_lowering=False, num_devices=1)
    arrays = {f"in_{k}": v for k, v in lay_out(inputs).items()}
    aps = {k[3:]: nc.dram_tensor(k, v.shape, mybir.dt.from_np(v.dtype), kind="ExternalInput").ap() for k, v in arrays.items()}
    out = nc.dram_tensor("out", (NSEQ, T, D), F32, kind="ExternalOutput").ap()
    build(nc, aps, out)
    return run_bass_kernel_spmd(nc, [arrays], core_ids=[0]).results[0]["out"]
```

```python
import numpy as np
import concourse.bass as bass
from concourse import mybir
from contextlib import ExitStack

F32 = mybir.dt.float32
F32R = mybir.dt.float32r
BF16 = mybir.dt.bfloat16
ALU = mybir.AluOpType
ACT = mybir.ActivationFunctionType
AX = mybir.AxisListType

P = 128
NL = 4
NSEQ = 16
T = 256
D = 256
H = 16
HD = D // H
DFF = 1024
NT = T // P
KD = D // P
NJ = DFF // P
HB = H // 2
STK = 48
ROWS = 64
RING = 4
STACKED = 16 * 2
SCRATCHED = 16 * 6
PRING = 8
NTILE = NL * NSEQ
SCALE = HD ** -0.5
MASKED = -1.0e30
EPS = (1e-5, 1e-5, 1e-5, float(np.finfo(np.float32).eps))
CAUSAL, ROPE = 1, 3
QKV_BIAS = (False, False, True, True)
WQ_COLS = (3 * D, 3 * D, 3 * D, 5 * D)
W1_COLS = (DFF, DFF, DFF, 2 * DFF)
V_SC1, V_SH1, V_SC2, V_SH2, V_G1, V_BE1, V_G2, V_BE2, V_BQ, V_BK, V_BV, V_BQR, V_BKR = range(0, 26, 2)
V_B1 = 26
V_T1 = 42
NVEC = 46
C_S1, C_B1, C_S2, C_B2 = 0, 2, 4, 6
SCORES_BY_UP = (1, 2, 3, 5, 6, 6, 9, 10)
MAXIMA_BY_HIDDEN = (1, 2, 3, 5, 6, 7, 9, 11)
DOWN_BEFORE = 6
S_BANKS = (4, 5, 4, 5, 0, 4, 5, 0, 4, 5, 0, 4, 5, 4, 5, 4)
ST_BANKS = ((4, 5, 1, 3) * 4, (4, 5, 4, 5, 1, 4, 5, 1) + (3, 4, 5, 1) * 2)
OUT = {6 + 4 * g + k: ("outputs", g, k) for g in range(3) for k in range(2)}
BETWEEN = ({0: ("values", 1, 0), 1: ("norm_2",), 16: ("values", 1, 1), **OUT},
           {0: ("down", 7, 0), 1: ("down", 7, 1), 3: ("norm_2",), 8: ("values", 0, 0), 9: ("values", 0, 1),
            12: ("values", 1, 0), 16: ("values", 1, 1), **OUT})
NORM2_AT = [[h for h, what in slots.items() if what == ("norm_2",)][0] for slots in BETWEEN]
CHUNK = 512
RAWS = 2
SPLIT_AT = (10, 11, 14, 15)


def build(nc, a, out):
    ctx = ExitStack()
    with ctx:
        def sb(name, shape, dt=F32):
            return ctx.enter_context(nc.sbuf_tensor(name, shape, dt))

        def sem(name):
            return ctx.enter_context(nc.semaphore(name))

        X = sb("X", [P, NSEQ, NT, D])
        IDENT = sb("IDENT", [P, P])
        IDENTB = sb("IDENTB", [P, P], BF16)
        MASK = sb("MASK", [P, 2, 2, T], BF16)
        ROT = sb("ROT", [P, 2, T])
        VEC = sb("VEC", [P, NL, NVEC])
        COND = sb("COND", [P, NL, 8, NSEQ])
        HALF = sb("HALF", [P, NT])
        WQ = [[sb(f"WQ{p}{x}", [P, KD, max(WQ_COLS[p::2])], F32R) for x in "hl"] for p in range(2)]
        WO = [sb(f"WO{x}", [P, KD, D], F32R) for x in "hl"]
        XQ = sb("XQ", [P, NT, D])
        TOK = sb("TOK", [P, NT, D])
        ST1, ST2 = sb("ST1", [P, NT, 6]), sb("ST2", [P, NT, 6])
        SPARE = sb("SPARE", [P, 1])
        MV1, MV2 = sb("MV1", [P, NT, 2]), sb("MV2", [P, NT, 2])
        RS1, RS2 = sb("RS1", [P, NT]), sb("RS2", [P, NT])
        TV = sb("TV", [P, NT])
        RAW = [sb(f"RAW{i}", [P, CHUNK]) for i in range(RAWS)]
        HF = sb("HF", [P, KD, T])
        H1 = [sb(f"H1{x}", [P, KD, T], F32R) for x in "hl"]
        H2 = [sb(f"H2{x}", [P, KD, T], F32R) for x in "hl"]
        QHL = sb("QHL", [P, 2, KD, T], F32R)
        KHL = sb("KHL", [P, 2, KD, T], F32R)
        QS = sb("QS", [P, HB, T], F32R)
        KS = sb("KS", [P, HB, T], F32R)
        V = sb("V", [P, NT, H, 32])
        NEGM = sb("NEGM", [P, NT, H])
        MT = sb("MT", [H, T], F32R)
        PR = sb("PR", [P, PRING, NT, T])
        OR = sb("OR", [P, 4, T])
        RZ = sb("RZ", [P, NT, H])
        G = sb("G", [P, RING, T])
        GH = [sb(f"GH{x}", [P, RING, T], F32R) for x in "hl"]
        GA = sb("GA", [P, 2, D])
        GM = sb("GM", [P, 2, D])
        B = ctx.enter_context(nc.psum_tensor("B", [P, 8, 512], F32))

        def bank(n, parts=2):
            return B[:, n, :].rearrange("p (a b) -> p a b", a=parts)

        sp_x = [sem(f"sp_x{half}") for half in range(2)]
        sp_const, sp_cw, sp_gs = sem("sp_const"), [sem(f"sp_cw{l}") for l in range(NL)], sem("sp_gs")
        sp_raw = [sem(f"sp_raw{i}") for i in range(RAWS)]
        sp_ga, sp_gm, sp_scr, sp_out = (sem("sp_" + x) for x in ("ga", "gm", "scr", "out"))
        sp_stk, sp_mt = [[sem(f"sp_{x}{half}") for half in range(2)] for x in ("stk", "mt")]
        pe_h1, pe_q, pe_k, pe_v, pe_s, pe_mt, pe_st, pe_pv, pe_ot1, pe_ot2, pe_wo, pe_h2, pe_up, pe_dn = (
            sem("pe_" + x) for x in ("h1", "q", "k", "v", "s", "mt", "st", "pv", "ot1", "ot2", "wo", "h2", "up", "dn"))
        ac_h1, ac_v, ac_mt, ac_exp, ac_o, ac_ot, ac_h2, ac_g, ac_w = (
            sem("ac_" + x) for x in ("h1", "v", "mt", "exp", "o", "ot", "h2", "g", "w"))
        dv_st1, dv_mv1, dv_xn1, dv_st2, dv_mv2, dv_xn2, dv_h1, dv_h2, dv_qh, dv_q, dv_kh, dv_k = (
            sem("dv_" + x) for x in ("st1", "mv1", "xn1", "st2", "mv2", "xn2", "h1", "h2", "qh", "q", "kh", "k"))
        dv_max, dv_rz, dv_on, dv_ot, dv_wo, dv_dn, dv_gh, dv_g, dv_rot, dv_rot2 = (
            sem("dv_" + x) for x in ("max", "rz", "on", "ot", "wo", "dn", "gh", "g", "rot", "rot2"))
        po_t1, po_rs1, po_t2, po_rs2, po_h1, po_h2, po_gl, po_xb1, po_x1, po_xb2, po_x2, po_w, po_init = (
            sem("po_" + x) for x in ("t1", "rs1", "t2", "rs2", "h1", "h2", "gl", "xb1", "x1", "xb2", "x2", "w", "init"))
        ac_table = sem("ac_table")
        cc, pt, ct, vz = sem("ac_silu"), sem("pe_t1"), sem("ac_t1"), sem("dv_t1")
        pg, vr, pm = sem("pe_gates"), sem("dv_rows"), sem("pe_modulation")
        dv_init = sem("dv_init")
        dv_w = sem("dv_w")

        q_scr = nc.dram_tensor("q_scratch", [3, HD, HB, KD, T], F32, kind="Internal").ap()
        k_scr = nc.dram_tensor("k_scratch", [3, HD, HB, KD, T], F32, kind="Internal").ap()
        g_scr = nc.dram_tensor("gate_scratch", [NL - 1, NSEQ, 4, D], F32, kind="Internal").ap()

        def columns(l, what):
            return {"q": WQ_COLS[l], "o": D, "1": W1_COLS[l], "2": D}[what]

        def chunks(l, what):
            n = columns(l, what)
            if n < CHUNK:
                k = CHUNK // n
                return [(slice(i, i + k), slice(0, n)) for i in range(0, NJ if what == "2" else KD, k)]
            step = max(c for c in range(1, CHUNK + 1) if n % c == 0)
            return [(slice(k, k + 1), slice(c, c + step)) for k in range(KD) for c in range(0, n, step)]

        order = [(l, what, *c) for l in range(NL) for what in "qo12" for c in chunks(l, what)]

        def numbers(l, what):
            return [n for n, c in enumerate(order) if c[0] == l and c[1] == what]

        def lows(n, vector):
            return sum((c[1] == "1") == vector for c in order[:n + 1])

        def hi_lo(n):
            l, what, k, c = order[n]
            both = WQ[l % 2] if what == "q" else WO if what == "o" else W1 if what == "1" else W2
            return [w[:, k, c] for w in both]

        def raw_view(n):
            l, what, k, c = order[n]
            parts, width = k.stop - k.start, c.stop - c.start
            return RAW[n % RAWS][:, 0:parts * width].rearrange("p (k n) -> p k n", k=parts)

        def load_raw(sp, ns):
            for n in ns:
                if n >= RAWS:
                    last = order[n - RAWS][1] == "1"
                    sp.wait_ge(dv_w if last else po_w, lows(n - RAWS, last))
                l, what, k, c = order[n]
                src = a[f"w{what}{l}"].rearrange("(k p) n -> p k n", p=P)
                sp.dma_start(raw_view(n), src[:, k, c]).then_inc(sp_raw[n % RAWS], 16)

        def split_hi(ac, n):
            ac.wait_ge(sp_raw[n % RAWS], 16 * (n // RAWS + 1))
            nc.scalar.activation(hi_lo(n)[0], raw_view(n), ACT.Copy).then_inc(ac_w, 1)

        def split_lo(eng, tensor_tensor, s_lo, l, what):
            for n in numbers(l, what):
                eng.wait_ge(ac_w, n + 1)
                hi, lo = hi_lo(n)
                tensor_tensor(lo, raw_view(n), hi.bitcast(F32), ALU.subtract).then_inc(s_lo, 1)

        with ExitStack() as early:
            def esb(name, shape, dt=F32):
                return early.enter_context(nc.sbuf_tensor(name, shape, dt))

            CW = [esb(f"CW{l}", [P, KD, 6 * D]) for l in range(3)]
            CT1 = X[:, 8:10, :, :].rearrange("p s t d -> p s (t d)")
            CT2 = X[:, 10:14, :, :].rearrange("p (k s) t d -> p k (s t d)", k=KD)
            CT = esb("CT", [P, KD, NSEQ])
            SC = esb("SC", [P, KD, NSEQ])
            SLU = esb("SLU", [P, KD, NSEQ])
            Z3 = esb("Z3", [P, KD, NSEQ])
            U = esb("U", [P, 2, NSEQ])
            U2 = esb("U2", [P, 2, NSEQ])
            flat = PR[:].rearrange("p a b c -> p (a b c)")
            GR = flat[0:NSEQ, 0:12 * D].rearrange("p (l r d) -> p l r d", l=NL - 1, r=4)
            RB = [flat[0:NSEQ, 12 * D:16 * D].rearrange("p (r d) -> p r d", r=4), OR[0:NSEQ], G[0:NSEQ]]
            block = early.enter_context(nc.Block())
            ctile = [bank(n, 32) for n in (0, 5, 6, 7)]
            t1tile = bank(1, 32)
            starts = [(D, 0, 4 * D, 3 * D)] * 3 + [(D, 0, 3 * D, 2 * D)]

            @block.sync
            def _(sp):
                x_in = a["x"].rearrange("s (t p) d -> p s t d", p=P)
                sp.dma_start(CT[:], a["c_t"]).then_inc(sp_cw[0], 16)
                sp.dma_start(VEC[:], a["vec"]).then_inc(sp_cw[0], 16)
                for l in range(3):
                    sp.dma_start(CW[l][:], a[f"cw{l}"].rearrange("(k p) n -> p k n", p=P)).then_inc(sp_cw[l], 16)
                    sp.dma_start(RB[l], a["rows"][l].partition_broadcast(NSEQ)).then_inc(sp_cw[l], 16)
                    if l == 0:
                        sp.dma_start(X[:, 0:8], x_in[:, 0:8]).then_inc(sp_x[0], 16)
                sp.dma_start(CT1, a["cw_t1"].rearrange("(k p) n -> p k n", p=P)).then_inc(sp_cw[ROPE], 16)
                sp.dma_start(CT2, a["cw_t2"].rearrange("(k p) n -> p k n", p=P)).then_inc(sp_cw[ROPE], 16)
                load_raw(sp, numbers(0, "q") + numbers(0, "o"))
                sp.dma_start(IDENT[:], a["ident"]).then_inc(sp_const, 16)
                sp.dma_start(ROT[:], a["rot"]).then_inc(sp_const, 16)
                sp.dma_start(MASK[:], a["mask"]).then_inc(sp_const, 16)
                sp.dma_start(IDENTB[:], a["ident_b"]).then_inc(sp_const, 16)
                sp.wait_ge(vr, 6)
                sp.dma_start(g_scr.rearrange("l s r d -> s l r d"), GR).then_inc(sp_gs, 16)
                sp.wait_ge(pm, NL)
                sp.dma_start(X[:, 8:16], x_in[:, 8:16]).then_inc(sp_x[1], 16)
                sp.wait_ge(sp_gs, 16)
                sp.wait_ge(sp_x[0], 16)
                sp.wait_ge(sp_const, 64)

            @block.gpsimd
            def _(po):
                nc.gpsimd.memset(HALF[:], -0.5).then_inc(po_init, 1)
                nc.gpsimd.memset(QS[:].bitcast(F32), 0.0).then_inc(po_init, 1)
                nc.gpsimd.memset(KS[:].bitcast(F32), 1.0).then_inc(po_init, 1)
                nc.gpsimd.memset(V[:], 0.0).then_inc(po_init, 1)
                split_lo(po, nc.gpsimd.tensor_tensor, po_w, 0, "q")
                split_lo(po, nc.gpsimd.tensor_tensor, po_w, 0, "o")
                po.wait_ge(po_init, 4)
                nc.gpsimd.memset(V[:, :, :, HD:HD + 1], 1.0).then_inc(po_init, 1)
                po.wait_ge(po_init, 5)

            @block.scalar
            def _(ac):
                ac.wait_ge(sp_cw[0], 16 * 4)
                nc.scalar.activation(SC[:], CT[:], ACT.Silu).then_inc(cc, 1)
                for n in numbers(0, "q"):
                    split_hi(ac, n)
                ac.wait_ge(pt, 1)
                for k in range(KD):
                    nc.scalar.activation(SLU[:, k, :], t1tile[:, KD + k, :], ACT.Silu,
                                         bias=VEC[:, ROPE, V_T1 + KD + k:V_T1 + KD + k + 1]).then_inc(ct, 1)
                for n in numbers(0, "o"):
                    split_hi(ac, n)

            @block.tensor
            def _(pe):
                pe.wait_ge(sp_cw[0], 16 * 4)
                pe.wait_ge(cc, 1)
                for l in range(NL):
                    if l > 0:
                        pe.wait_ge(sp_cw[l], 32)
                    if l == ROPE:
                        for f in range(2 * KD):
                            for k in range(KD):
                                last = nc.tensor.matmul(t1tile[:, f, :], CT1[:, k, f * P:(f + 1) * P], CT[:, k, :],
                                                        start=(k == 0), stop=(k == KD - 1))
                        last.then_inc(pt, 1)
                        pe.wait_ge(vz, KD)
                    else:
                        for r, c0 in enumerate((2 * D, 5 * D)):
                            for k in range(KD):
                                last = nc.tensor.matmul(bank(2 + l)[0:NSEQ, r, :], SC[:, k, :], CW[l][:, k, c0:c0 + D],
                                                        start=(k == 0), stop=(k == KD - 1))
                        last.then_inc(pg, 1)
                    w, m = (CT2, Z3) if l == ROPE else (CW[l], SC)
                    for c, c0 in enumerate(starts[l]):
                        for f in range(KD):
                            for k in range(KD):
                                last = nc.tensor.matmul(ctile[l][:, 2 * c + f, :],
                                                        w[:, k, c0 + f * P:c0 + (f + 1) * P], m[:, k, :],
                                                        start=(k == 0), stop=(k == KD - 1))
                    last.then_inc(pm, 1)

            @block.vector
            def _(dv):
                n = [0]

                def chain(ins):
                    n[0] += 1
                    ins.then_inc(dv_init, 1)

                def settle():
                    dv.wait_ge(dv_init, n[0])

                for l in range(NL):
                    if l == ROPE:
                        dv.wait_ge(ct, KD)
                        for k in range(KD):
                            nc.vector.scalar_tensor_tensor(Z3[:, k, :], t1tile[:, k, :], VEC[:, ROPE, V_T1 + k:V_T1 + k + 1],
                                                           SLU[:, k, :], ALU.add, ALU.mult).then_inc(vz, 1)
                    else:
                        dv.wait_ge(pg, 1 + l)
                        for r in range(2):
                            chain(nc.vector.tensor_tensor(GR[:, l, 2 * r, :], bank(2 + l)[0:NSEQ, r, :],
                                                          RB[l][:, 2 * r, :], ALU.add))
                        settle()
                        for r in range(2):
                            nc.vector.tensor_tensor(GR[:, l, 2 * r + 1, :], GR[:, l, 2 * r, :], RB[l][:, 2 * r + 1, :],
                                                    ALU.mult).then_inc(vr, 1)
                    dv.wait_ge(pm, 1 + l)
                    for half, (sc, sh, g, be, cs, cb) in enumerate(((V_SC1, V_SH1, V_G1, V_BE1, C_S1, C_B1),
                                                                   (V_SC2, V_SH2, V_G2, V_BE2, C_S2, C_B2))):
                        for f in range(KD):
                            def vec(c):
                                return VEC[:, l, c + f:c + f + 1]
                            tile = 4 * half + f
                            chain(nc.vector.tensor_scalar(U[:, f, :], ctile[l][:, tile, :], vec(sc), 1.0, ALU.add, ALU.add))
                            chain(nc.vector.tensor_scalar(U2[:, f, :], ctile[l][:, tile + KD, :], vec(sh), None, ALU.add))
                            settle()
                            chain(nc.vector.tensor_scalar(COND[:, l, cs + f, :], U[:, f, :], vec(g), None, ALU.mult))
                            chain(nc.vector.scalar_tensor_tensor(COND[:, l, cb + f, :], U[:, f, :], vec(be), U2[:, f, :],
                                                                 ALU.mult, ALU.add))
                            settle()

        W1 = [sb(f"W1{x}", [P, KD, 2 * DFF], F32R) for x in "hl"]
        W2 = [sb(f"W2{x}", [P, NJ, D], F32R) for x in "hl"]

        class Step:

            def __init__(self, t, layer):
                fixed = isinstance(t, int)
                self.first = fixed and t == -2

                def stage(tile):
                    there = not fixed or 0 <= tile < NTILE
                    l = tile // NSEQ if fixed else layer
                    before = max(0, min(tile, NTILE)) if fixed else tile
                    return tile if there else None, l, tile - NSEQ * l, before, before + there

                self.n, self.ln, self.sn, self.nn, self.n_done = stage(t + 2)
                self.q, self.lq, self.sq, self.nq, self.q_done = stage(t + 1)
                self.a, self.la, self.sa, self.na, self.a_done = stage(t)
                self.r, self.lr, self.sr, self.nr, self.r_done = stage(t - 1)
                self.m, self.lm, self.sm, self.nm, self.m_done = stage(t - 2)
                self.table_m = (t - 1) // NSEQ if fixed else layer
                self.conv_q = self.conv_o = self.conv_12 = None
                if fixed:
                    if t == 0:
                        self.conv_12 = 0
                    elif t % NSEQ == NSEQ - 2 and 0 < t < NTILE - 2:
                        self.conv_q = t // NSEQ + 1
                    elif t % NSEQ == 0 and 0 < t < NTILE:
                        self.conv_o = t // NSEQ
                    elif t % NSEQ == 1 and 1 < t < NTILE:
                        self.conv_12 = t // NSEQ

            def new_weights(self, numbers):
                return [n for l, kinds in ((self.conv_q, "q"), (self.conv_o, "o"), (self.conv_12, "12")) if l is not None
                        for what in kinds for n in numbers(l, what)]

        def seq(s):
            return slice(s, s + 1) if isinstance(s, int) else bass.ds(s, 1)

        def at_least(eng, s, value):
            if not isinstance(value, int) or value > 0:
                eng.wait_ge(s, value)

        def apart(eng):
            eng.nop(nofuse=True)

        def hidden_hi(eng, s, j):
            if s.lm == ROPE:
                eng.wait_ge(dv_gh, NJ * (s.m - NSEQ * ROPE) + j + 1)
            else:
                eng.wait_ge(ac_g, NJ * s.m + j + 1)

        def last_user(banks, h):
            return max((g for g in range(h) if banks[g] == banks[h]), default=None)

        def steps(eng, body):
            t = -2
            for l in range(NL):
                lo = NSEQ * l + 2 + (l in (0, ROPE))
                hi = NSEQ * l + NSEQ - 2
                while t < lo:
                    body(Step(t, None))
                    t += 1
                with eng.Fori(lo, hi) as i:
                    body(Step(i, l))
                t = hi
            while t < NTILE + 2:
                body(Step(t, None))
                t += 1

        block = ctx.enter_context(nc.Block())

        @block.tensor
        def _(pe):
            def product(dst, w, x, first_k, last_k):
                for n, (i, j) in enumerate(((0, 0), (0, 1), (1, 0))):
                    last = nc.tensor.matmul(dst, w[i], x[j], start=(first_k and n == 0), stop=(last_k and n == 2))
                return last

            def project(dst, w, x):
                for k in range(KD):
                    last = product(dst, [v[:, k] for v in w], [v[:, k] for v in x], k == 0, k == KD - 1)
                return last

            def cols(w, c):
                return [v[:, :, c:c + P] for v in w]

            def weights(l, what):
                n = numbers(l, what)[-1]
                pe.wait_ge(ac_w, n + 1)
                pe.wait_ge(dv_w if what == "1" else po_w, lows(n, what == "1"))

            def body(s):
                def scores(h):
                    a_, b = s.a, ROWS * (h // HB)
                    if h == 0:
                        at_least(pe, ac_exp, H * s.na)
                    if h % HB == 0:
                        pe.wait_ge(sp_stk[h // HB], STACKED * (a_ + 1))
                    before = last_user(S_BANKS, h)
                    if before is not None:
                        pe.wait_ge(dv_max, H * a_ + before + 1)
                    elif S_BANKS[h] == 0:
                        at_least(pe, dv_on, 2 * s.r_done)
                        at_least(pe, ac_h2, s.nr)
                        at_least(pe, dv_q, s.nq)
                    for i in range(NT):
                        dst = bank(S_BANKS[h])[:, i, :]
                        last = nc.tensor.matmul(dst, QS[b:b + STK, h % HB, i * P:(i + 1) * P], KS[b:b + STK, h % HB, :],
                                                start=True, stop=(s.la != CAUSAL))
                        if s.la == CAUSAL:
                            last = nc.tensor.matmul(dst, IDENTB[:], MASK[:, 0, i, :], start=False, stop=True)
                    last.then_inc(pe_s, 1)

                def up(j):
                    m, dst = s.m, bank(3 - j % 2)
                    if j == 0:
                        weights(s.lm, "1")
                        pe.wait_ge(dv_h2, m + 1)
                        pe.wait_ge(po_h2, m + 1)
                        at_least(pe, dv_k, s.nq)
                    elif j == 1:
                        at_least(pe, dv_k, s.nq)
                        at_least(pe, ac_v, s.nq)
                    elif s.lm == ROPE:
                        pe.wait_ge(dv_g, NJ * (m - NSEQ * ROPE) + j - 1)
                    else:
                        pe.wait_ge(ac_g, NJ * m + j - 1)
                    last = project(dst[:, 0, :], cols(W1, j * P), H2)
                    if s.lm == ROPE:
                        last = project(dst[:, 1, :], cols(W1, DFF + j * P), H2)
                    last.then_inc(pe_up, 1)

                def down(j, tiles=range(NT)):
                    m = s.m
                    if j == 0:
                        weights(s.lm, "2")
                        at_least(pe, dv_wo, s.r_done)
                        at_least(pe, ac_o, 2 * s.na)
                    hidden_hi(pe, s, j)
                    pe.wait_ge(po_gl, NJ * m + j + 1)
                    for i in tiles:
                        for n, (x, y) in enumerate(((0, 0), (0, 1), (1, 0))):
                            last = nc.tensor.matmul(bank(7)[:, i, :], GH[x][:, j % RING, i * P:(i + 1) * P],
                                                    W2[y][:, j, :], start=(j == 0 and n == 0 and i == 0),
                                                    stop=(j == NJ - 1 and n == 2), skip_group_check=True)
                    if i == NT - 1:
                        last.then_inc(pe_dn, 1)

                def to_features(dst, src):
                    for f in range(KD):
                        for i in range(NT):
                            last = nc.tensor.transpose(dst[:, f, i * P:(i + 1) * P], src[:, i, f * P:(f + 1) * P], IDENT[:])
                    return last

                def outputs_to_tokens():
                    pe.wait_ge(ac_o, 2 * s.r + 2)
                    at_least(pe, ac_h2, s.nr)
                    at_least(pe, dv_q, s.nq)
                    for i in range(NT):
                        for g in range(4):
                            last = nc.tensor.transpose(bank(i, 4)[:, g, :], OR[:, g, i * P:(i + 1) * P], IDENT[:])
                        last.then_inc(pe_ot1, 1)

                def outputs_to_features():
                    pe.wait_ge(dv_on, 2 * s.r + 2)
                    to_features(bank(6), TOK).then_inc(pe_ot2, 1)

                def output_projection():
                    weights(s.lr, "o")
                    pe.wait_ge(ac_ot, s.r + 1)
                    pe.wait_ge(dv_ot, s.r + 1)
                    for i in range(NT):
                        for k in range(KD):
                            last = product(bank(7)[:, i, :], [x[:, k, i * P:(i + 1) * P] for x in H1],
                                           [w[:, k, :] for w in WO], k == 0, k == KD - 1)
                    last.then_inc(pe_wo, 1)

                def norm_1():
                    pe.wait_ge(dv_xn1, s.q + 1)
                    at_least(pe, dv_q, s.nq)
                    at_least(pe, dv_on, 2 * s.r_done)
                    to_features(bank(1), XQ).then_inc(pe_h1, 1)

                def norm_2():
                    at_least(pe, dv_q, s.q_done)
                    pe.wait_ge(dv_xn2, s.r + 1)
                    to_features(bank(0), TOK).then_inc(pe_h2, 1)

                def early_scores(upto):
                    while s.a is not None and at[0] < upto:
                        scores(at[0])
                        at[0] += 1

                at = [0]
                for j in range(NJ):
                    if j == 5 and s.q is not None:
                        norm_1()
                    if s.m is not None:
                        up(j)
                    if s.r is not None:
                        if j == 2:
                            outputs_to_features()
                        if j == 4:
                            output_projection()
                    early_scores(SCORES_BY_UP[j])
                    if s.r is not None and j == 0:
                        outputs_to_tokens()
                    if s.m is not None and j >= 5:
                        down(j - 5 if j == 5 else j - 4)
                        if j == 5:
                            early_scores(7)
                            down(1)
                if s.m is not None:
                    early_scores(12)
                    down(4)
                    for j in range(DOWN_BEFORE, NJ) if s.a is None else ():
                        down(j)
                wq, rope = WQ[s.lq % 2], s.lq == ROPE
                early_scores(13)
                for f in range(KD):
                    if s.q is not None:
                        if f == 0:
                            weights(s.lq, "q")
                            pe.wait_ge(dv_h1, s.q + 1)
                            pe.wait_ge(po_h1, s.q + 1)
                            if rope:
                                at_least(pe, ac_h2, s.nr)
                                if s.a is not None:
                                    pe.wait_ge(dv_max, H * s.a + last_user(S_BANKS + (0,), H) + 1)
                        last = project(bank(1)[:, f, :], cols(wq, f * P), H1)
                        if rope:
                            last = project(bank(0)[:, f, :], cols(wq, 3 * D + f * P), H1)
                        if f == KD - 1:
                            last.then_inc(pe_q, 1)
                    early_scores(14 + f)
                if s.m is not None:
                    down(5)
                early_scores(H)
                if s.q is not None:
                    if s.m is not None:
                        if s.lm == ROPE:
                            pe.wait_ge(dv_g, NJ * (s.m - NSEQ * ROPE) + NJ)
                        else:
                            pe.wait_ge(ac_g, NJ * s.m + NJ)
                    at_least(pe, ac_v, s.nq)
                    at_least(pe, dv_k, s.nq)
                    project(bank(3)[:, 0, :], cols(wq, D), H1)
                if s.a is not None:
                    pe.wait_ge(dv_max, H * s.a + H)
                    at_least(pe, ac_ot, s.r_done)
                    at_least(pe, dv_ot, s.r_done)
                    for i in range(NT):
                        last = nc.tensor.transpose(B[0:H, 6, i * P:(i + 1) * P], NEGM[:, i, :], IDENT[:])
                    last.then_inc(pe_mt, 1)
                if s.q is not None:
                    last = project(bank(3)[:, 1, :], cols(wq, D + P), H1)
                    if rope:
                        for f in range(KD):
                            last = project(bank(2)[:, f, :], cols(wq, 4 * D + f * P), H1)
                    last.then_inc(pe_k, 1)

                def values(i, k):
                    if rope and i == k == 0:
                        pe.wait_ge(dv_k, s.q + 1)
                    last = product(bank(2)[:, i, :], [x[:, k, i * P:(i + 1) * P] for x in H1],
                                   [w[:, k, 2 * D:3 * D] for w in wq], k == 0, k == KD - 1)
                    if i == NT - 1 and k == KD - 1:
                        last.then_inc(pe_v, 1)

                if s.q is not None and s.a is None:
                    for i in range(NT):
                        for k in range(KD):
                            values(i, k)

                if s.a is not None:
                    a_ = s.a

                    def outputs(g, k):
                        pe.wait_ge(ac_exp, H * a_ + 4 * g + 4)
                        if g == 0:
                            pe.wait_ge(ac_v, a_ + 1)
                            pe.wait_ge(ac_mt, a_ + 1)
                        if g == 2:
                            at_least(pe, dv_dn, s.m_done)
                        for j in range(4):
                            h = 4 * g + j
                            last = nc.tensor.matmul(bank(6 + g // 2)[32 * j:32 * j + 32, g % 2, :],
                                                    V[:, k, h, :], PR[:, h % PRING, k, :],
                                                    start=(k == 0), stop=(k == NT - 1))
                        if k == NT - 1:
                            last.then_inc(pe_pv, 1)

                    if s.m is not None:
                        down(DOWN_BEFORE)
                        if not rope:
                            down(DOWN_BEFORE + 1)
                    if s.q is not None and not rope:
                        values(0, 0)
                        values(0, 1)
                    for h in range(H):
                        if h % HB == 0:
                            pe.wait_ge(sp_mt[h // HB], 16 * (a_ + 1))
                        b = ROWS * (h // HB)
                        before = last_user(ST_BANKS[rope], h)
                        if before is not None:
                            pe.wait_ge(ac_exp, H * a_ + before + 1)
                        elif ST_BANKS[rope][h] == 1:
                            pe.wait_ge(dv_q, s.q_done)
                        elif ST_BANKS[rope][h] == 3:
                            pe.wait_ge(dv_k, s.q_done)
                        for k in range(NT):
                            dst = bank(ST_BANKS[rope][h])[:, k, :]
                            last = nc.tensor.matmul(dst, KS[b:b + ROWS, h % HB, k * P:(k + 1) * P],
                                                    QS[b:b + ROWS, h % HB, :], start=True, stop=(s.la != CAUSAL))
                            if s.la == CAUSAL:
                                last = nc.tensor.matmul(dst, IDENTB[:], MASK[:, 1, k, :], start=False, stop=True)
                        last.then_inc(pe_st, 1)
                        what, *which = BETWEEN[rope].get(h, (None,))
                        if what == "outputs":
                            outputs(*which)
                        elif what == "values" and s.q is not None:
                            values(*which)
                        elif what == "down" and s.m is not None:
                            down(which[0], which[1:])
                        elif what == "norm_2" and s.r is not None:
                            norm_2()
                    if s.q is not None:
                        values(*BETWEEN[rope][H][1:])
                    for k in range(NT):
                        outputs(3, k)
                elif s.r is not None:
                    norm_2()
            steps(pe, body)

        @block.scalar
        def _(ac):
            def table(function):
                nc.scalar.activation(SPARE[:], HALF[:, 0:1], function).then_inc(ac_table, 1)

            def cond(s, layer, sequence, c):
                return COND[:, layer, c, seq(sequence)]

            def body(s):
                splits = s.new_weights(numbers)
                if s.m is None:
                    if s.r is not None:
                        outputs_hi(s)
                    modulate(s, s.q, s.lq, s.sq, 0)
                for j in range(NJ) if s.m is not None else ():
                    m = s.m
                    ac.wait_ge(pe_up, NJ * m + j + 1)
                    if j == 0:
                        at_least(ac, dv_k, s.nq)
                    at_least(ac, po_gl, NJ * m + j + 1 - RING)
                    if s.lm == ROPE:
                        nc.scalar.activation(G[:, j % RING, :], bank(3 - j % 2)[:, 1, :], ACT.Silu,
                                             bias=VEC[:, ROPE, V_B1 + NJ + j:V_B1 + NJ + j + 1]).then_inc(ac_g, 1)
                    else:
                        at_least(ac, pe_dn, NJ * m + j + 1 - RING)
                        for dst in (G, GH[0]):
                            last = nc.scalar.activation(dst[:, j % RING, :], bank(3 - j % 2)[:, 0, :], ACT.Gelu,
                                                        bias=VEC[:, s.lm, V_B1 + j:V_B1 + j + 1])
                        last.then_inc(ac_g, 1)
                    if j == 2 and s.r is not None:
                        outputs_hi(s)
                    if j == 5:
                        modulate(s, s.q, s.lq, s.sq, 0)
                if s.a is None:
                    modulate(s, s.r, s.lr, s.sr, 1)
                if s.a is not None:
                    a_ = s.a
                    ac.wait_ge(pe_mt, a_ + 1)
                    for half in range(2):
                        at_least(ac, sp_mt[half], 16 * s.na)
                    nc.scalar.activation(MT[:], B[0:H, 6, 0:T], ACT.Copy).then_inc(ac_mt, 1)
                    table(ACT.Exp)
                    for h in range(H):
                        ac.wait_ge(pe_st, H * a_ + h + 1)
                        at_least(ac, pe_pv, 4 * a_ + h // 4 - 1)
                        nc.scalar.activation(PR[:, h % PRING, :, :], bank(ST_BANKS[s.lq == ROPE][h]), ACT.Exp,
                                             scale=SCALE).then_inc(ac_exp, 1)
                        if h in SPLIT_AT and splits:
                            split_hi(ac, splits.pop(0))
                        norm2_at = NORM2_AT[s.lq == ROPE]
                        if h in (norm2_at + 2, norm2_at + 4):
                            modulate(s, s.r, s.lr, s.sr, 1, (h - norm2_at) // 2 - 1)
                        if h == 12:
                            evacuate(s, 0)
                    table(ACT.Silu if s.table_m == ROPE else ACT.Gelu)
                    evacuate(s, 1)
                if s.q is not None:
                    ac.wait_ge(pe_v, s.q + 1)
                    at_least(ac, pe_pv, 4 * s.a_done)
                    nc.scalar.activation(V[:, :, :, 0:HD], B[:, 2, :].rearrange("p (i h d) -> p i h d", i=NT, h=H),
                                         ACT.Copy).then_inc(ac_v, 1)
                for n in splits:
                    split_hi(ac, n)

            def outputs_hi(s):
                ac.wait_ge(pe_ot2, s.r + 1)
                at_least(ac, pe_v, s.nq)
                for f in range(KD):
                    if QKV_BIAS[s.lr]:
                        last = nc.scalar.activation(H1[0][:, f, :], bank(6)[:, f, :], ACT.Identity,
                                                    bias=VEC[:, s.lr, V_BV + f:V_BV + f + 1])
                    else:
                        last = nc.scalar.activation(H1[0][:, f, :], bank(6)[:, f, :], ACT.Copy)
                last.then_inc(ac_ot, 1)

            def evacuate(s, half):
                ac.wait_ge(pe_pv, 4 * s.a + 2 * half + 2)
                at_least(ac, pe_ot1, 2 * s.r_done)
                nc.scalar.activation(OR[:, 2 * half:2 * half + 2, :], bank(6 + half), ACT.Copy).then_inc(ac_o, 1)

            def modulate(s, tile, layer, sequence, second, only=None):
                if tile is None:
                    return
                if second:
                    nbank, sc, sh, s_pe, s_ac = 0, C_S2, C_B2, pe_h2, ac_h2
                    at_least(ac, dv_h1, s.q_done)
                    at_least(ac, po_h1, s.q_done)
                else:
                    nbank, sc, sh, s_pe, s_ac = 1, C_S1, C_B1, pe_h1, ac_h1
                    at_least(ac, dv_h2, s.nr)
                    at_least(ac, po_h2, s.nr)
                ac.wait_ge(s_pe, tile + 1)
                for f in range(KD) if only is None else (only,):
                    last = nc.scalar.activation(HF[:, f, :], bank(nbank)[:, f, :], ACT.Identity,
                                                bias=cond(s, layer, sequence, sh + f), scale=cond(s, layer, sequence, sc + f))
                if f == KD - 1:
                    last.then_inc(s_ac, 1)

            steps(ac, body)

        @block.vector
        def _(dv):
            def statistics(x, st, mv, s_st, s_mv, n):
                for i in range(NT):
                    last = nc.vector.bn_stats(st[:, i, :], x[i])
                last.then_inc(s_st, 1)
                dv.wait_ge(s_st, n + 1)
                apart(dv)
                for i in range(NT):
                    last = nc.vector.bn_aggr(mv[:, i, :], st[:, i, :])
                last.then_inc(s_mv, 1)

            def normalise(dst, x, mv, rs, s_xn, rms):
                for i in range(NT):
                    if rms:
                        last = nc.vector.tensor_scalar(dst[:, i, :], x[i], rs[:, i:i + 1], None, ALU.mult)
                    else:
                        last = nc.vector.tensor_scalar(dst[:, i, :], x[i], mv[:, i, 0:1], rs[:, i:i + 1],
                                                       ALU.subtract, ALU.mult)
                last.then_inc(s_xn, 1)

            def tokens(sequence):
                return [X[:, seq(sequence), i, :] for i in range(NT)]

            def body(s):
                def maximum(h):
                    a_ = s.a
                    dv.wait_ge(pe_s, H * a_ + h + 1)
                    if h == 0:
                        at_least(dv, pe_mt, s.na)
                    nc.vector.tensor_reduce(NEGM[:, :, h], bank(S_BANKS[h]), op=ALU.max, axis=AX.X,
                                            negate=True).then_inc(dv_max, 1)

                def hidden(j):
                    m = s.m
                    if s.lm == ROPE:
                        dv.wait_ge(ac_g, NJ * m + j + 1)
                        nc.vector.scalar_tensor_tensor(G[:, j % RING, :], bank(3 - j % 2)[:, 0, :],
                                                       VEC[:, ROPE, V_B1 + j:V_B1 + j + 1], G[:, j % RING, :],
                                                       ALU.add, ALU.mult).then_inc(dv_g, 1)
                        dv.wait_ge(dv_g, NJ * (m - NSEQ * ROPE) + j + 1)
                        at_least(dv, pe_dn, NJ * m + j + 1 - RING)
                        nc.vector.tensor_copy(GH[0][:, j % RING, :], G[:, j % RING, :]).then_inc(dv_gh, 1)

                at = [0]

                def early_maxima(upto):
                    while s.a is not None and at[0] < upto:
                        maximum(at[0])
                        at[0] += 1

                def split_1():
                    if s.q is None:
                        return
                    dv.wait_ge(ac_h1, s.q + 1)
                    at_least(dv, pe_v, s.nq)
                    at_least(dv, pe_wo, s.r_done)
                    nc.vector.tensor_copy(H1[0][:], HF[:]).then_inc(dv_h1, 1)

                def normalised_outputs():
                    at_least(dv, po_x2, s.nm)
                    for i in range(NT):
                        dv.wait_ge(pe_ot1, 2 * s.r + i + 1)
                        heads = B[:, i, :].rearrange("p (h c) -> p h c", h=H)
                        nc.vector.reciprocal(RZ[:, i, :], heads[:, :, HD]).then_inc(dv_rz, 1)
                        dv.wait_ge(dv_rz, 2 * s.r + i + 1)
                        nc.vector.tensor_tensor(TOK[:, i, :].rearrange("p (h d) -> p h d", h=H), heads[:, :, 0:HD],
                                                RZ[:, i, :].unsqueeze(2).to_broadcast([P, H, HD]),
                                                ALU.mult).then_inc(dv_on, 1)

                def outputs_lo():
                    dv.wait_ge(ac_ot, s.r + 1)
                    if QKV_BIAS[s.lr]:
                        for f in range(KD):
                            last = nc.vector.scalar_tensor_tensor(H1[1][:, f, :], bank(6)[:, f, :],
                                                                  VEC[:, s.lr, V_BV + f:V_BV + f + 1],
                                                                  H1[0][:, f, :].bitcast(F32), ALU.add, ALU.subtract)
                    else:
                        last = nc.vector.tensor_tensor(H1[1][:], bank(6), H1[0][:].bitcast(F32), ALU.subtract)
                    last.then_inc(dv_ot, 1)

                early_maxima(1)
                if s.r is not None:
                    normalised_outputs()
                for j in range(NJ):
                    early_maxima(MAXIMA_BY_HIDDEN[j])
                    if s.m is not None:
                        hidden(j)
                    if s.r is not None:
                        if j == 2:
                            outputs_lo()
                        if j == 3:
                            dv.wait_ge(pe_wo, s.r + 1)
                            multiply(s, bank(7), GA, sp_ga, s.r, s.lr).then_inc(dv_wo, 1)
                    if j == 5:
                        split_1()
                early_maxima(H)
                if s.r is not None:
                    dv.wait_ge(po_x1, s.r + 1)
                    statistics(tokens(s.sr), ST2, MV2, dv_st2, dv_mv2, s.r)
                if s.q is not None:
                    split_qk(s, pe_q, QHL, 1, 0, V_BQ, V_BQR, dv_qh, dv_q, 0)
                if s.r is not None:
                    dv.wait_ge(po_rs2, s.r + 1)
                    normalise(TOK, tokens(s.sr), MV2, RS2, dv_xn2, s.lr == ROPE)
                if s.q is not None:
                    split_qk(s, pe_k, KHL, 3, 2, V_BK, V_BKR, dv_kh, dv_k, 1)
                if s.r is not None:
                    dv.wait_ge(ac_h2, s.r + 1)
                    at_least(dv, pe_up, NJ * s.m_done)
                    nc.vector.tensor_copy(H2[0][:], HF[:]).then_inc(dv_h2, 1)
                if s.m is not None:
                    dv.wait_ge(pe_dn, NJ * s.m + NJ)
                    at_least(dv, pe_h2, s.r_done)
                    multiply(s, bank(7), GM, sp_gm, s.m, s.lm).then_inc(dv_dn, 1)
                if s.n is not None:
                    if isinstance(s.n, int) and s.n == 4:
                        dv.wait_ge(sp_x[1], 16)
                    if s.ln > 0:
                        dv.wait_ge(po_x2, s.n - (NSEQ - 1))
                    statistics(tokens(s.sn), ST1, MV1, dv_st1, dv_mv1, s.n)
                    dv.wait_ge(po_rs1, s.n + 1)
                    at_least(dv, pe_h1, s.q_done)
                    normalise(XQ, tokens(s.sn), MV1, RS1, dv_xn1, s.ln == ROPE)
                if s.conv_12 is not None:
                    split_lo(dv, nc.vector.tensor_tensor, dv_w, s.conv_12, "1")

            def multiply(s, src, rows, s_rows, n, layer):
                if layer == ROPE:
                    return nc.vector.tensor_copy(TOK[:], src)
                dv.wait_ge(s_rows, 16 * (n + 1))
                return nc.vector.tensor_tensor(TOK[:], src, rows[:, 0:1, :].to_broadcast([P, NT, D]), ALU.mult)

            def split_qk(s, s_pe, dst, nbank, nswap, vb, vbr, s_hi, s_lo, which):
                dv.wait_ge(s_pe, s.q + 1)
                at_least(dv, sp_scr, SCRATCHED * s.nq)
                if s.lq == ROPE:
                    if s.m is not None:
                        dv.wait_ge(po_gl, NJ * s.m_done)
                    if which == 1:
                        dv.wait_ge(dv_q, s.q + 1)
                    r = s.q - NSEQ * ROPE
                    for c, nb, b in ((0, nbank, vb), (1, nswap, vbr)):
                        for f in range(KD):
                            last = nc.vector.scalar_tensor_tensor(G[:, 2 * c + f, :], bank(nb)[:, f, :],
                                                                  VEC[:, ROPE, b + f:b + f + 1], ROT[:, c, :],
                                                                  ALU.add, ALU.mult)
                    last.then_inc(dv_rot, 1)
                    dv.wait_ge(dv_rot, 2 * r + which + 1)
                    nc.vector.tensor_tensor(G[:, 0:2, :], G[:, 0:2, :], G[:, 2:4, :], ALU.add).then_inc(dv_rot2, 1)
                    dv.wait_ge(dv_rot2, 2 * r + which + 1)
                    nc.vector.tensor_copy(dst[:, 0], G[:, 0:2, :]).then_inc(s_hi, 1)
                    dv.wait_ge(s_hi, s.q + 1)
                    nc.vector.tensor_tensor(dst[:, 1], G[:, 0:2, :], dst[:, 0].bitcast(F32), ALU.subtract).then_inc(s_lo, 1)
                elif QKV_BIAS[s.lq]:
                    for f in range(KD):
                        last = nc.vector.tensor_scalar(dst[:, 0, f, :], bank(nbank)[:, f, :],
                                                       VEC[:, s.lq, vb + f:vb + f + 1], None, ALU.add)
                    last.then_inc(s_hi, 1)
                    dv.wait_ge(s_hi, s.q + 1)
                    for f in range(KD):
                        last = nc.vector.scalar_tensor_tensor(dst[:, 1, f, :], bank(nbank)[:, f, :],
                                                              VEC[:, s.lq, vb + f:vb + f + 1],
                                                              dst[:, 0, f, :].bitcast(F32), ALU.add, ALU.subtract)
                    last.then_inc(s_lo, 1)
                else:
                    nc.vector.tensor_copy(dst[:, 0], bank(nbank)).then_inc(s_hi, 1)
                    dv.wait_ge(s_hi, s.q + 1)
                    nc.vector.tensor_tensor(dst[:, 1], bank(nbank), dst[:, 0].bitcast(F32), ALU.subtract).then_inc(s_lo, 1)

            steps(dv, body)

        @block.gpsimd
        def _(po):
            def rstd(mv, rs, s_mv, s_t, s_rs, n, layer):
                po.wait_ge(s_mv, n + 1)
                if layer == ROPE:
                    nc.gpsimd.tensor_tensor(TV[:], mv[:, :, 0], mv[:, :, 0], ALU.mult).then_inc(s_t, 1)
                    po.wait_ge(s_t, n + 2 * (n - NSEQ * ROPE) + 1)
                    nc.gpsimd.tensor_tensor(TV[:], TV[:], mv[:, :, 1], ALU.add).then_inc(s_t, 1)
                    po.wait_ge(s_t, n + 2 * (n - NSEQ * ROPE) + 2)
                    apart(po)
                    nc.gpsimd.tensor_scalar(TV[:], TV[:], EPS[layer], None, ALU.add).then_inc(s_t, 1)
                    po.wait_ge(s_t, n + 2 * (n - NSEQ * ROPE) + 3)
                else:
                    apart(po)
                    nc.gpsimd.tensor_scalar(TV[:], mv[:, :, 1], EPS[layer], None, ALU.add).then_inc(s_t, 1)
                    po.wait_ge(s_t, n + 1)
                nc.gpsimd.tensor_tensor(rs[:], TV[:], HALF[:], ALU.pow).then_inc(s_rs, 1)

            def bias_rows(layer, n):
                return not (layer == 0 and n == 0)

            def x_of(sequence):
                return X[:, seq(sequence), :, :].rearrange("p a t d -> p (a t) d")

            def residual_1(s):
                x = x_of(s.sr)
                po.wait_ge(dv_xn1, s.r + 1)
                po.wait_ge(sp_ga, 16 * (s.r + 1))
                apart(po)
                nc.gpsimd.tensor_tensor(x, x, GA[:, 1:2, :].to_broadcast([P, NT, D]), ALU.add).then_inc(po_xb1, 1)
                po.wait_ge(po_xb1, s.r + 1)
                po.wait_ge(dv_wo, s.r + 1)
                apart(po)
                nc.gpsimd.tensor_tensor(x, x, TOK[:], ALU.add).then_inc(po_x1, 1)

            def body(s):
                for j in range(NJ):
                    if s.m is not None:
                        hidden_hi(po, s, j)
                        nc.gpsimd.tensor_tensor(GH[1][:, j % RING, :], G[:, j % RING, :], GH[0][:, j % RING, :].bitcast(F32),
                                                ALU.subtract).then_inc(po_gl, 1)
                    if j == 2 and s.r is not None:
                        residual_1(s)
                    if j == 5:
                        low_1(s)
                if s.r is not None:
                    rstd(MV2, RS2, dv_mv2, po_t2, po_rs2, s.r, s.lr)
                    po.wait_ge(ac_h2, s.r + 1)
                    po.wait_ge(dv_h2, s.r + 1)
                    nc.gpsimd.tensor_tensor(H2[1][:], HF[:], H2[0][:].bitcast(F32), ALU.subtract).then_inc(po_h2, 1)
                if s.m is not None:
                    m, xm = s.m, x_of(s.sm)
                    po.wait_ge(dv_xn2, m + 1)
                    po.wait_ge(sp_gm, 16 * (m + 1))
                    apart(po)
                    nc.gpsimd.tensor_tensor(xm, xm, GM[:, 1:2, :].to_broadcast([P, NT, D]), ALU.add).then_inc(po_xb2, 1)
                    po.wait_ge(po_xb2, m + 1)
                    po.wait_ge(dv_dn, m + 1)
                    apart(po)
                    nc.gpsimd.tensor_tensor(xm, xm, TOK[:], ALU.add).then_inc(po_x2, 1)
                if s.n is not None:
                    rstd(MV1, RS1, dv_mv1, po_t1, po_rs1, s.n, s.ln)
                if s.conv_q is not None:
                    split_lo(po, nc.gpsimd.tensor_tensor, po_w, s.conv_q, "q")
                if s.conv_o is not None:
                    split_lo(po, nc.gpsimd.tensor_tensor, po_w, s.conv_o, "o")
                if s.conv_12 is not None:
                    split_lo(po, nc.gpsimd.tensor_tensor, po_w, s.conv_12, "2")

            def low_1(s):
                if s.q is None:
                    return
                po.wait_ge(dv_h1, s.q + 1)
                nc.gpsimd.tensor_tensor(H1[1][:], HF[:], H1[0][:].bitcast(F32), ALU.subtract).then_inc(po_h1, 1)

            steps(po, body)

        @block.sync
        def _(sp):
            def hold(s, value):
                at_least(sp, s, value)
                apart(sp)

            def rows(dst, layer, sequence, half):
                if layer == ROPE:
                    return dst[:], a["rows_last"][half].partition_broadcast(P)
                src = g_scr[layer, seq(sequence), 2 * half:2 * half + 2, :].rearrange("a r d -> (a r) d")
                return dst[:], src.partition_broadcast(P)

            def store(s, tile, sequence):
                hold(po_x2, tile + 1)
                o = out[seq(sequence), :, :].rearrange("a (t p) d -> p (a t) d", p=P)
                sp.dma_start(o, X[:, seq(sequence), :, :].rearrange("p a t d -> p (a t) d")).then_inc(sp_out, 16)

            def body(s):
                if s.r is not None:
                    hold(dv_wo, s.nr)
                    hold(po_xb1, s.nr)
                    sp.dma_start(*rows(GA, s.lr, s.sr, 0)).then_inc(sp_ga, 16)
                if s.m is not None:
                    hold(dv_dn, s.nm)
                    hold(po_xb2, s.nm)
                    sp.dma_start(*rows(GM, s.lm, s.sm, 1)).then_inc(sp_gm, 16)
                    if s.lm == ROPE and not (isinstance(s.m, int) and s.m == NSEQ * ROPE):
                        store(s, s.m - 1, s.sm - 1)
                if s.a is not None:
                    hold(ac_mt, s.a + 1)
                    for half in range(2):
                        row = ROWS * half + STK
                        sp.dma_start(QS[row:row + 1, :, :].bitcast(F32),
                                     MT[HB * half:HB * half + HB, :].bitcast(F32)).then_inc(sp_mt[half], 16)
                loads = s.new_weights(numbers)
                if s.conv_12:
                    hold(pe_up, NJ * NSEQ * s.conv_12)
                    hold(pe_dn, NJ * NSEQ * s.conv_12)
                load_raw(sp, loads[:RAWS])
                if s.q is not None:
                    for half in range(2):
                        hold(sp_stk[half], STACKED * s.nq)
                    for s_dv, src, scr, ranks in ((dv_q, QHL, q_scr, (0, 1, 0)), (dv_k, KHL, k_scr, (0, 0, 1))):
                        hold(s_dv, s.q + 1)
                        for r, x in enumerate(ranks):
                            sp.dma_start(scr[r].rearrange("d h f n -> h d (f n)"),
                                         src[:, x].rearrange("p f n -> p (f n)").bitcast(F32)).then_inc(sp_scr, 16)
                    hold(sp_scr, SCRATCHED * (s.q + 1))
                    for half in range(2):
                        if s.a is not None:
                            if half == 1:
                                load_raw(sp, loads[RAWS:2 * RAWS])
                            hold(pe_st, H * s.a + HB * (half + 1))
                        for scr, dst in ((q_scr, QS), (k_scr, KS)):
                            b = ROWS * half
                            sp.dma_start(dst[b:b + STK, :, :].bitcast(F32),
                                         scr[:, :, :, half, :].rearrange("r d h n -> (r d) h n")).then_inc(sp_stk[half], 16)

                load_raw(sp, loads[RAWS if s.q is None or s.a is None else 2 * RAWS:])

            steps(sp, body)
            store(None, NTILE - 1, NSEQ - 1)
            sp.wait_ge(sp_out, 16 * NSEQ)


def lay_out(i):
    g = {k: np.asarray(v) for k, v in i.items()}
    d = {"x": g["x"]}

    def cols(v):
        return np.asarray(v).reshape(-1, P).T

    d["c_t"] = np.ascontiguousarray(g["cond_1024"].T.reshape(KD, P, NSEQ).transpose(1, 0, 2))
    d["cw0"], d["cw1"], d["cw2"] = g["L0_cond_wc"].T, g["L1_cond_Wada"], g["L2_cond_Wt"]
    d["cw_t1"], d["cw_t2"] = g["L3_cond_w_t1"], g["L3_cond_w_t2"]
    rep = H // 4

    def spread(w):
        return np.repeat(w.T.reshape(D, 4, 1, HD), rep, axis=2).reshape(D, D)

    swap = np.arange(D).reshape(-1, 2)[:, ::-1].reshape(-1)
    w3 = g["L3_cond_w_qkv"]
    d["wq0"] = np.concatenate([g["L0_cond_wq"].T, spread(g["L0_cond_wk"]), spread(g["L0_cond_wv"])], axis=1)
    d["wq1"], d["wq2"] = g["L1_cond_Wqkv"], g["L2_cond_Wqkv"]
    d["wq3"] = np.concatenate([w3, w3[:, 0:D][:, swap], w3[:, D:2 * D][:, swap]], axis=1)
    d["wo0"], d["wo1"], d["wo2"], d["wo3"] = g["L0_cond_wo"].T, g["L1_cond_Wproj"], g["L2_cond_Wproj"], g["L3_cond_w_ao"]
    d["w10"], d["w11"], d["w12"], d["w13"] = g["L0_cond_w1"].T, g["L1_cond_W1"], g["L2_cond_W1"], g["L3_cond_w_fc"]
    d["w20"], d["w21"], d["w22"], d["w23"] = g["L0_cond_w2"].T, g["L1_cond_W2"], g["L2_cond_W2"], g["L3_cond_w_fo"]

    one, none = np.ones(D, np.float32), np.zeros(D, np.float32)
    vec = np.zeros((P, NL, NVEC), np.float32)

    def put(l, c, v):
        v = cols(v)
        vec[:, l, c:c + v.shape[1]] = v

    mod = [g["L0_cond_bc"], g["L1_cond_bada"], g["L2_cond_bt"]]
    for l in range(3):
        b = mod[l].reshape(6, D)
        for c, v in ((V_SH1, b[0]), (V_SC1, b[1]), (V_SH2, b[3]), (V_SC2, b[4])):
            put(l, c, v)
    b = g["L3_cond_b_t2"].reshape(4, D)
    for c, v in ((V_SH1, b[0]), (V_SC1, b[1]), (V_SH2, b[2]), (V_SC2, b[3])):
        put(3, c, v)
    norms = [(one, none, one, none)] + [tuple(g[f"L{l}_cond_{n}"] for n in ("g1", "be1", "g2", "be2")) for l in (1, 2)] + [
        (g["L3_cond_g1"], none, g["L3_cond_g2"], none)]
    for l, vs in enumerate(norms):
        for c, v in zip((V_G1, V_BE1, V_G2, V_BE2), vs):
            put(l, c, v)
    for l, bq in ((2, g["L2_cond_bqkv"]), (3, g["L3_cond_b_qkv"])):
        for c, v in zip((V_BQ, V_BK, V_BV), bq.reshape(3, D)):
            put(l, c, v)
    put(3, V_BQR, g["L3_cond_b_qkv"][0:D][swap])
    put(3, V_BKR, g["L3_cond_b_qkv"][D:2 * D][swap])
    for l, v in enumerate((g["L0_cond_b1"], g["L1_cond_b1"], g["L2_cond_b1"], g["L3_cond_b_fc"])):
        put(l, V_B1, v)
    put(3, V_T1, g["L3_cond_b_t1"])
    d["vec"] = vec
    outs = [(none, g["L0_cond_b2"]), (g["L1_cond_bproj"], g["L1_cond_b2"]), (g["L2_cond_bproj"], g["L2_cond_b2"])]
    d["rows"] = np.stack([np.stack([mod[l][2 * D:3 * D], outs[l][0], mod[l][5 * D:6 * D], outs[l][1]]) for l in range(3)])
    d["rows_last"] = np.stack([np.stack([v, v]) for v in (g["L3_cond_b_ao"], g["L3_cond_b_fo"])])

    d["ident"] = np.eye(P, dtype=np.float32)
    d["ident_b"] = np.eye(P, dtype=np.dtype("bfloat16"))
    freq = np.float32(1.0) / np.float32(10000.0) ** (np.arange(0, HD, 2, dtype=np.float32) / np.float32(HD))
    ang = (np.arange(T, dtype=np.float32)[:, None] * freq[None, :]).astype(np.float32)
    f = np.arange(P) % HD
    sign = np.where(f % 2 == 0, -1.0, 1.0).astype(np.float32)
    d["rot"] = np.stack([np.cos(ang).T[f // 2], np.sin(ang).T[f // 2] * sign[:, None]], axis=1).astype(np.float32)
    row, col = np.arange(P)[:, None], np.arange(T)[None, :]
    mask = np.zeros((P, 2, 2, T), np.float32)
    for i in range(2):
        mask[:, 0, i] = np.where(col > i * P + row, MASKED, 0.0)
        mask[:, 1, i] = np.where(i * P + row > col, MASKED, 0.0)
    d["mask"] = mask.astype(np.dtype("bfloat16"))
    return {k: np.ascontiguousarray(v) for k, v in d.items()}


def kernel(**inputs):
    import concourse.bacc as bacc
    from concourse.bass_utils import run_bass_kernel_spmd

    nc = bacc.Bacc("TRN2", target_bir_lowering=False, num_devices=1)
    arrays = {f"in_{k}": v for k, v in lay_out(inputs).items()}
    aps = {k[3:]: nc.dram_tensor(k, v.shape, mybir.dt.from_np(v.dtype), kind="ExternalInput").ap() for k, v in arrays.items()}
    out = nc.dram_tensor("out", (NSEQ, T, D), F32, kind="ExternalOutput").ap()
    build(nc, aps, out)
    return run_bass_kernel_spmd(nc, [arrays], core_ids=[0]).results[0]["out"]
```
